# Optimizing a Trainium2 kernel written in Bass

```python
import numpy as np
import jax
import jax.numpy as jnp

def _softmax(x, axis=-1):
    return jax.nn.softmax(x, axis=axis)

def _gelu(x):
    return jax.nn.gelu(x, approximate=True)

def _silu(x):
    return jax.nn.silu(x)

def _sigmoid(x):
    return jax.nn.sigmoid(x)

def _layernorm(x, axis=-1, eps=1e-05):
    m = jnp.mean(x, axis=axis, keepdims=True)
    v = jnp.var(x, axis=axis, keepdims=True)
    return (x - m) / jnp.sqrt(v + eps)

def _scatter_add(tgt, idx, src, axis=0):
    return tgt.at[idx].add(src)

def _segment_sum(src, seg, n):
    return jax.ops.segment_sum(src, seg, n)
kernel_name = 'mk_lm_tower_d1_tok_ids256_r4_3bbff8'

def setup_inputs(seed: int=0):
    np.random.seed(seed)
    _w = jnp.asarray

    def _rec_inputs():
        import jax
        import jax.numpy as jnp
        _rk = jax.random.key(seed)
        x = jax.random.randint(jax.random.fold_in(_rk, 1), (16, 512), 0, 12564, jnp.int32)
        return x
    x = _rec_inputs()

    def _L0_tok_setup():
        import jax, jax.numpy as jnp
        import numpy as np
        INP_SIZE = 50257
        HIDDEN = 64
        KSIZE = 9
        B, T = (16, 1024)
        key = jax.random.key(seed)
        k1, k2, k3, k4 = jax.random.split(key, 4)
        x = jax.random.randint(k1, (B, T), 0, INP_SIZE, dtype=jnp.int64 if jax.config.jax_enable_x64 else jnp.int32)
        emb = jax.random.normal(k2, (INP_SIZE, HIDDEN), dtype=jnp.float32) * 0.02
        fan_in = HIDDEN * KSIZE
        bound = 1.0 / np.sqrt(fan_in)
        W = jax.random.uniform(k3, (HIDDEN, HIDDEN, KSIZE), dtype=jnp.float32, minval=-bound, maxval=bound)
        b = jax.random.uniform(k4, (HIDDEN,), dtype=jnp.float32, minval=-bound, maxval=bound)
        return {'x': x, 'emb': emb, 'W': W, 'b': b}
    _L0_tok_all = _L0_tok_setup()
    _L0_tok_in = {k: v for k, v in _L0_tok_all.items() if k in ('emb', 'W', 'b')}
    del _L0_tok_all

    def _L0_attn_setup():
        import jax, jax.numpy as jnp
        import numpy as np
        B, T, F, H = (128, 256, 64, 128)

        def _lstm(xWb, U, reverse=False, return_sequences=False):
            Hn = U.shape[0]
            xs = jnp.swapaxes(xWb, 0, 1)
            h0 = jnp.zeros((xWb.shape[0], Hn), xWb.dtype)
            c0 = h0

            def step(carry, xw):
                h, c = carry
                z = xw + h @ U
                i, f, g, o = jnp.split(z, 4, axis=-1)
                i = jax.nn.sigmoid(i)
                f = jax.nn.sigmoid(f)
                g = jnp.tanh(g)
                o = jax.nn.sigmoid(o)
                c = f * c + i * g
                h = o * jnp.tanh(c)
                return ((h, c), h)
            (hT, _), hs = jax.lax.scan(step, (h0, c0), xs, reverse=reverse)
            if return_sequences:
                return jnp.swapaxes(hs, 0, 1)
            return hT
        key = jax.random.key(seed)
        ks = jax.random.split(key, 9)
        g = lambda k, shape: jax.random.normal(k, shape, jnp.float32) * 0.05
        return {'x': jax.random.uniform(ks[0], (B, T, F), jnp.float32), 'Wf': g(ks[1], (F, 4 * H)), 'Uf': g(ks[2], (H, 4 * H)), 'bf': jnp.zeros((4 * H,), jnp.float32), 'Wb': g(ks[3], (F, 4 * H)), 'Ub': g(ks[4], (H, 4 * H)), 'bb': jnp.zeros((4 * H,), jnp.float32), 'Wd': g(ks[5], (2 * H, 4 * H)), 'Ud': g(ks[6], (H, 4 * H)), 'bd': jnp.zeros((4 * H,), jnp.float32), 'Wo': g(ks[7], (H, F)), 'bo': jnp.zeros((F,), jnp.float32)}
    _L0_attn_all = _L0_attn_setup()
    _L0_attn_in = {k: v for k, v in _L0_attn_all.items() if k in ('Wf', 'Uf', 'bf', 'Wb', 'Ub', 'bb', 'Wd', 'Ud', 'bd', 'Wo', 'bo')}
    del _L0_attn_all

    def _L0_ffn_setup():
        import jax, jax.numpy as jnp
        import numpy as np
        E, D, H, TOP_K = (6, 64, 64, 2)
        ROUTER_H = D // 2
        key = jax.random.key(seed)
        ks = jax.random.split(key, 12)
        s = 1.0 / np.sqrt(D)
        sh = 1.0 / np.sqrt(H)
        sr = 1.0 / np.sqrt(ROUTER_H)
        return {'features': jax.random.normal(ks[0], (8, 1024, D), dtype=jnp.float32), 'router_w1': jax.random.uniform(ks[1], (D, ROUTER_H), jnp.float32, -s, s), 'router_b1': jnp.zeros((ROUTER_H,), jnp.float32), 'router_w2': jax.random.uniform(ks[2], (ROUTER_H, E), jnp.float32, -sr, sr), 'router_b2': jnp.zeros((E,), jnp.float32), 'expert_w1': jax.random.uniform(ks[3], (E, D, H), jnp.float32, -s, s), 'expert_b1': jnp.zeros((E, H), jnp.float32), 'expert_w2': jax.random.uniform(ks[4], (E, H, H), jnp.float32, -sh, sh), 'expert_b2': jnp.zeros((E, H), jnp.float32), 'expert_w3': jax.random.uniform(ks[5], (E, H, D), jnp.float32, -sh, sh), 'expert_b3': jnp.zeros((E, D), jnp.float32)}
    _L0_ffn_all = _L0_ffn_setup()
    _L0_ffn_in = {k: v for k, v in _L0_ffn_all.items() if k in ('router_w1', 'router_b1', 'router_w2', 'router_b2', 'expert_w1', 'expert_b1', 'expert_w2', 'expert_b2', 'expert_w3', 'expert_b3')}
    del _L0_ffn_all
    return {'x': x, 'L0_tok_emb': _L0_tok_in['emb'], 'L0_tok_W': _L0_tok_in['W'], 'L0_tok_b': _L0_tok_in['b'], 'L0_attn_Wf': _L0_attn_in['Wf'], 'L0_attn_Uf': _L0_attn_in['Uf'], 'L0_attn_bf': _L0_attn_in['bf'], 'L0_attn_Wb': _L0_attn_in['Wb'], 'L0_attn_Ub': _L0_attn_in['Ub'], 'L0_attn_bb': _L0_attn_in['bb'], 'L0_attn_Wd': _L0_attn_in['Wd'], 'L0_attn_Ud': _L0_attn_in['Ud'], 'L0_attn_bd': _L0_attn_in['bd'], 'L0_attn_Wo': _L0_attn_in['Wo'], 'L0_attn_bo': _L0_attn_in['bo'], 'L0_ffn_router_w1': _L0_ffn_in['router_w1'], 'L0_ffn_router_b1': _L0_ffn_in['router_b1'], 'L0_ffn_router_w2': _L0_ffn_in['router_w2'], 'L0_ffn_router_b2': _L0_ffn_in['router_b2'], 'L0_ffn_expert_w1': _L0_ffn_in['expert_w1'], 'L0_ffn_expert_b1': _L0_ffn_in['expert_b1'], 'L0_ffn_expert_w2': _L0_ffn_in['expert_w2'], 'L0_ffn_expert_b2': _L0_ffn_in['expert_b2'], 'L0_ffn_expert_w3': _L0_ffn_in['expert_w3'], 'L0_ffn_expert_b3': _L0_ffn_in['expert_b3']}

def reference(x, L0_tok_emb, L0_tok_W, L0_tok_b, L0_attn_Wf, L0_attn_Uf, L0_attn_bf, L0_attn_Wb, L0_attn_Ub, L0_attn_bb, L0_attn_Wd, L0_attn_Ud, L0_attn_bd, L0_attn_Wo, L0_attn_bo, L0_ffn_router_w1, L0_ffn_router_b1, L0_ffn_router_w2, L0_ffn_router_b2, L0_ffn_expert_w1, L0_ffn_expert_b1, L0_ffn_expert_w2, L0_ffn_expert_b2, L0_ffn_expert_w3, L0_ffn_expert_b3):
    import jax
    import jax.numpy as jnp

    def _L0_tok_ref(x, emb, W, b):
        import jax, jax.numpy as jnp
        import numpy as np
        INP_SIZE = 50257
        HIDDEN = 64
        KSIZE = 9
        B, T = (16, 1024)
        offsets = jnp.arange(-(KSIZE // 2), KSIZE // 2 + 1)
        idx = jnp.clip(x[..., None] + offsets, 0, INP_SIZE - 1)
        gathered = emb[idx]
        out = jnp.einsum('btkh,ohk->bto', gathered, W) + b
        return out

    def _L0_attn_ref(x, Wf, Uf, bf, Wb, Ub, bb, Wd, Ud, bd, Wo, bo):
        import jax, jax.numpy as jnp
        import numpy as np
        B, T, F, H = (128, 256, 64, 128)

        def _lstm(xWb, U, reverse=False, return_sequences=False):
            Hn = U.shape[0]
            xs = jnp.swapaxes(xWb, 0, 1)
            h0 = jnp.zeros((xWb.shape[0], Hn), xWb.dtype)
            c0 = h0

            def step(carry, xw):
                h, c = carry
                z = xw + h @ U
                i, f, g, o = jnp.split(z, 4, axis=-1)
                i = jax.nn.sigmoid(i)
                f = jax.nn.sigmoid(f)
                g = jnp.tanh(g)
                o = jax.nn.sigmoid(o)
                c = f * c + i * g
                h = o * jnp.tanh(c)
                return ((h, c), h)
            (hT, _), hs = jax.lax.scan(step, (h0, c0), xs, reverse=reverse)
            if return_sequences:
                return jnp.swapaxes(hs, 0, 1)
            return hT
        h_fwd = _lstm(x @ Wf + bf, Uf, reverse=False)
        h_bwd = _lstm(x @ Wb + bb, Ub, reverse=True)
        latent = jnp.concatenate([h_fwd, h_bwd], axis=-1)
        rep = jnp.broadcast_to(latent[:, None, :], (x.shape[0], x.shape[1], 2 * H))
        dec = _lstm(rep @ Wd + bd, Ud, return_sequences=True)
        return dec @ Wo + bo

    def _L0_ffn_ref(features, router_w1, router_b1, router_w2, router_b2, expert_w1, expert_b1, expert_w2, expert_b2, expert_w3, expert_b3):
        import jax, jax.numpy as jnp
        import numpy as np
        E, D, H, TOP_K = (6, 64, 64, 2)
        ROUTER_H = D // 2
        rh = jax.nn.relu(features @ router_w1 + router_b1)
        expert_logits = jax.nn.softmax(rh @ router_w2 + router_b2, axis=-1)
        top_w, top_i = jax.lax.top_k(expert_logits, TOP_K)
        routing_weights = jax.nn.softmax(top_w, axis=-1)
        h1 = jax.nn.relu(jnp.einsum('bsd,edh->bseh', features, expert_w1) + expert_b1)
        h2 = jax.nn.relu(jnp.einsum('bseh,ehf->bsef', h1, expert_w2) + expert_b2)
        expert_out = jnp.einsum('bsef,efo->bseo', h2, expert_w3) + expert_b3
        sel = jnp.take_along_axis(expert_out, top_i[:, :, :, None], axis=2)
        combined = jnp.sum(sel * routing_weights[..., None], axis=2)
        return combined
    h = _L0_tok_ref(x, L0_tok_emb, L0_tok_W, L0_tok_b)
    h = h + _L0_attn_ref(_layernorm(h, axis=-1), L0_attn_Wf, L0_attn_Uf, L0_attn_bf, L0_attn_Wb, L0_attn_Ub, L0_attn_bb, L0_attn_Wd, L0_attn_Ud, L0_attn_bd, L0_attn_Wo, L0_attn_bo)
    h = h + _L0_ffn_ref(_layernorm(h, axis=-1), L0_ffn_router_w1, L0_ffn_router_b1, L0_ffn_router_w2, L0_ffn_router_b2, L0_ffn_expert_w1, L0_ffn_expert_b1, L0_ffn_expert_w2, L0_ffn_expert_b2, L0_ffn_expert_w3, L0_ffn_expert_b3)
    return h

_drawn_inputs = setup_inputs


def setup_inputs(seed=0):
    import zlib

    import numpy as np

    out = dict(_drawn_inputs(seed))
    spreads = {'L0_attn_bf': (0.0, 0.1),
     'L0_attn_bb': (0.0, 0.1),
     'L0_attn_bd': (0.0, 0.1),
     'L0_attn_bo': (0.0, 0.1),
     'L0_ffn_router_b1': (0.0, 0.1),
     'L0_ffn_router_b2': (0.0, 0.1),
     'L0_ffn_expert_b1': (0.0, 0.1),
     'L0_ffn_expert_b2': (0.0, 0.1),
     'L0_ffn_expert_b3': (0.0, 0.1)}
    factors = {}
    for name, (base, spread) in spreads.items():
        noise = np.random.default_rng([zlib.crc32(name.encode()), seed]).standard_normal(out[name].shape)
        drawn = base * np.exp(spread * noise) if base else spread * noise
        out[name] = jnp.asarray(drawn.astype(out[name].dtype))
    for name, factor in factors.items():
        out[name] = (out[name] * factor).astype(out[name].dtype)
    return out
```

```python
from contextlib import ExitStack

import concourse.bass as bass
from concourse import mybir

F32 = mybir.dt.float32
F16 = mybir.dt.float16
BF16 = mybir.dt.bfloat16
I32 = mybir.dt.int32
U32 = mybir.dt.uint32
ALU = mybir.AluOpType
ACT = mybir.ActivationFunctionType

B, T = 16, 512
D = 64
KS = 9
H = 128
NE = 6
RH = 32
VOCAB = 50257
HALF = KS // 2
PAD = 2 * HALF
P = 128
STEPS = P // B
NCH = T // STEPS
SEED = STEPS // 2
GK = KS * D
NK = (GK + P - 1) // P
PAIRS = NE // 2
NPAD = 8
EPS = 1e-5
S = 256.0
LEAST = -1.0e30


def tower(nc, ids, table, conv_w, conv_b, w_in, u_in, b_in, wd, ud, bd, wo, bo,
          r_w1, r_b1, r_w2, r_b2, e_w1, e_b1, e_w2, e_b2, e_w3, e_b3, out):
    with ExitStack() as ctx:
        def sb(name, shape, dt=F32):
            return ctx.enter_context(nc.sbuf_tensor(name, shape, dt))

        def bank(name, dt=F32):
            return ctx.enter_context(nc.psum_tensor(name, [P, 2048 // (4 if dt == F32 else 2)], dt))

        def sem(name):
            return ctx.enter_context(nc.semaphore(name))

        raw = sb("raw", [P, 8, 4 * H])
        hi = sb("hi", [P, 8, 4 * H], F16)
        lo = sb("lo", [P, 8, 4 * H], F16)
        brow = sb("brow", [P, 4, 4 * H])
        brest = sb("brest", [P, 4, 4 * H])
        bp_hi = sb("bp_hi", [P, 4, 4 * H], BF16)
        bp_mid = sb("bp_mid", [P, 4, 4 * H], BF16)
        bpart = sb("bpart", [P, 4, 4 * H], BF16)
        ones = sb("ones", [P, P], BF16)
        ident = sb("ident", [P, P])
        ident16 = sb("ident16", [P, P], F16)
        convw = sb("convw", [P, NK, D])
        convb = sb("convb", [P, D])
        bob = sb("bob", [P, D])
        cb = sb("cb", [P, D])
        w1 = sb("w1", [P, PAIRS + 1, P])
        w2 = sb("w2", [P, PAIRS, P])
        b2 = sb("b2", [P, PAIRS])
        w3 = sb("w3", [P, PAIRS, P])
        wr2 = sb("wr2", [P, NPAD])
        iota = sb("iota", [P, NPAD])
        halfneg = sb("halfneg", [P, 1])
        idx_in = sb("idx_in", [P, NCH], I32)
        idx_f = sb("idx_f", [P, NCH])
        idx = sb("idx", [P, NCH], I32)
        rows = sb("rows", [P, 2, GK])
        rowsT = sb("rowsT", [P, NK * P])
        h1 = sb("h1", [P, NCH, D])
        hx = sb("hx", [P, 2, D])
        st = sb("st", [P, 6])
        mv = sb("mv", [P, 2])
        ve = sb("ve", [P, 1])
        rstd = sb("rstd", [P, 1])
        xn32 = sb("xn32", [P, D])
        xn = sb("xn", [P, 2 * D], F16)
        xT = sb("xT", [P, (NCH + 2) * P], F16)
        gates = [sb(f"gates{d}", [P, 2, 4 * B]) for d in "fb"]
        tho = [sb(f"tho{d}", [P, B]) for d in "fb"]
        prod = [sb(f"prod{d}", [P, 2 * B]) for d in "fb"]
        tc = [sb(f"tc{d}", [P, B]) for d in "fb"]
        h32 = [sb(f"h32{d}", [P, B]) for d in "fb"]
        hhi = [sb(f"hhi{d}", [P, STEPS, B], F16) for d in "fb"]
        hlo = [sb(f"hlo{d}", [P, STEPS, B], F16) for d in "fb"]
        zc32 = sb("zc32", [P, 4 * B])
        zc_hi = sb("zc_hi", [P, SEED, 4 * B], F16)
        zc_lo = sb("zc_lo", [P, SEED, 4 * B], F16)
        y1 = sb("y1", [P, D])
        yres = sb("yres", [P, D])
        acc = sb("acc", [P, D])
        yout = sb("yout", [P, D])
        fx = sb("fx", [P, P])
        fxT = sb("fxT", [P, P])
        g1 = sb("g1", [P, PAIRS + 1, P])
        g2 = sb("g2", [P, PAIRS, P])
        m8 = sb("m8", [P, NPAD])
        dl = sb("dl", [P, NPAD])
        ex = sb("ex", [P, NPAD])
        exs = sb("exs", [P, 1])
        exr = sb("exr", [P, 1])
        pr = sb("pr", [P, NPAD])
        p8 = sb("p8", [P, NPAD])
        top = sb("top", [P, NPAD], U32)
        topf = sb("topf", [P, NPAD])
        pd = sb("pd", [P, 1])
        pe_ = sb("pe_", [P, 1])
        pden = sb("pden", [P, 1])
        wt0 = sb("wt0", [P, 1])
        wt1 = sb("wt1", [P, 1])
        rw0 = sb("rw0", [P, NPAD])
        rw1 = sb("rw1", [P, NPAD])
        rw = sb("rw", [P, NPAD])

        z_ifg = [bank("z_ifg_f"), bank("z_ifg_b")]
        z_o = [bank("z_o_f"), bank("z_o_b")]
        pA, pB, pC, pD = bank("pA"), bank("pB"), bank("pC"), bank("pD")

        s_ids = sem("s_ids")
        s_conv = sem("s_conv")
        s_small = sem("s_small")
        s_lstm = sem("s_lstm")
        s_ffw = sem("s_ffw")
        s_const = sem("s_const")
        s_idx = sem("s_idx")
        s_prep = sem("s_prep")
        s_rows = [sem("s_rows0"), sem("s_rows1")]
        s_tr = sem("s_tr")
        s_trA = sem("s_trA")
        s_trB = sem("s_trB")
        s_conv_mm = sem("s_conv_mm")
        s_h1 = sem("s_h1")
        s_st = sem("s_st")
        s_mv = sem("s_mv")
        s_ve = sem("s_ve")
        s_rstd = sem("s_rstd")
        s_xn = sem("s_xn")
        s_xn32 = sem("s_xn32")
        s_xnT = sem("s_xnT")
        s_xT = sem("s_xT")
        zi = [sem("zi_f"), sem("zi_b")]
        zo = [sem("zo_f"), sem("zo_b")]
        ai = [sem("ai_f"), sem("ai_b")]
        ao = [sem("ao_f"), sem("ao_b")]
        at = [sem("at_f"), sem("at_b")]
        dp = [sem("dp_f"), sem("dp_b")]
        dc = [sem("dc_f"), sem("dc_b")]
        dhi = [sem("dhi_f"), sem("dhi_b")]
        dh = [sem("dh_f"), sem("dh_b")]
        dlo = [sem("dlo_f"), sem("dlo_b")]
        s_zc = sem("s_zc")
        s_zcs = sem("s_zcs")
        dzi, dzo, dai, dao, dat = sem("dzi"), sem("dzo"), sem("dai"), sem("dao"), sem("dat")
        ddp, ddc, ddhi, ddh, ddlo = sem("ddp"), sem("ddc"), sem("ddhi"), sem("ddh"), sem("ddlo")
        f_proj = sem("f_proj")
        f_y1 = sem("f_y1")
        f_st = sem("f_st")
        f_mv = sem("f_mv")
        f_ve = sem("f_ve")
        f_rstd = sem("f_rstd")
        f_fx = sem("f_fx")
        f_tr = sem("f_tr")
        f_fxT = sem("f_fxT")
        f_l1 = sem("f_l1")
        f_g1 = sem("f_g1")
        f_lg = sem("f_lg")
        f_l2 = sem("f_l2")
        f_g2 = sem("f_g2")
        f_l3 = sem("f_l3")
        f_route = [sem(f"f_route{k}") for k in range(1, ROUTE + 1)]
        f_ex = sem("f_ex")
        f_pe = sem("f_pe")
        f_yres = sem("f_yres")
        f_comb = sem("f_comb")
        s_out = sem("s_out")

        block = ctx.enter_context(nc.Block())

        UF, UB, UD, WF, WB, WDF, WDB, WO = range(8)
        FACT = {UF: S / 4, UB: S / 4, UD: S / 4, WF: S / 2, WB: S / 2, WDF: S / 4, WDB: S / 4, WO: S / 2}
        ENC_B, DEC_B, E3_B = (0, 1), 2, 3
        G = slice(2 * H, 3 * H)
        SMALL = 16 * 10
        FFW = 16 * 11

        @block.sync
        def _(sp):
            sp.dma_start(idx_in[:], ids).then_inc(s_ids, 16)
            cw = conv_w.rearrange("k h o -> (k h) o")
            sp.dma_start(convw[:, 0:NK - 1, :], cw[0:(NK - 1) * P, :].rearrange("(m p) o -> p m o", p=P)).then_inc(s_conv, 16)
            sp.dma_start(convw[0:GK - (NK - 1) * P, NK - 1, :], cw[(NK - 1) * P:GK, :]).then_inc(s_conv, 16)
            sp.dma_start(convb[:], conv_b.rearrange("(a d) -> a d", a=1).broadcast_to([P, D])).then_inc(s_conv, 16)
            sp.dma_start(bob[:], bo.rearrange("(a d) -> a d", a=1).broadcast_to([P, D])).then_inc(s_conv, 16)
            for j, w in ((UF, u_in[0]), (UB, u_in[1]), (UD, ud)):
                sp.dma_start(raw[:, j, :], w).then_inc(s_lstm, 16)
            for j, w in ((WF, w_in[0]), (WB, w_in[1])):
                for q in range(2):
                    sp.dma_start(raw[q * D:(q + 1) * D, j, :], w).then_inc(s_lstm, 16)
            sp.dma_start(raw[:, WDF, :], wd[0:H, :]).then_inc(s_lstm, 16)
            sp.dma_start(raw[:, WDB, :], wd[H:2 * H, :]).then_inc(s_lstm, 16)
            sp.dma_start(raw[:, WO, 0:D], wo).then_inc(s_lstm, 16)
            sp.wait_ge(s_const, 6)
            for q in (0, 32, 64):
                for j, b in enumerate((b_in[0], b_in[1], bd)):
                    sp.dma_start(brow[q:q + 1, j, :], b.rearrange("(a n) -> a n", a=1)).then_inc(s_small, 16)
                sp.dma_start(brow[q:q + 1, E3_B, 0:NE * D], e_b3.rearrange("(a e) d -> a (e d)", a=1)).then_inc(s_small, 16)
            sp.dma_start(w1[0:D, 0:PAIRS, :].rearrange("p j (q h) -> p (j q) h", q=2), e_w1.rearrange("e d h -> d e h")).then_inc(s_ffw, 16)
            sp.dma_start(w1[D:D + 1, 0:PAIRS, :].rearrange("p j c -> p (j c)"), e_b1.rearrange("(a e) h -> a (e h)", a=1)).then_inc(s_ffw, 16)
            sp.dma_start(w1[0:D, PAIRS, 0:RH], r_w1).then_inc(s_ffw, 16)
            sp.dma_start(w1[D:D + 1, PAIRS, 0:RH], r_b1.rearrange("(a n) -> a n", a=1)).then_inc(s_ffw, 16)
            for q in range(2):
                sp.dma_start(w2[q * D:(q + 1) * D, :, q * D:(q + 1) * D], e_w2.rearrange("(j q) h f -> q h j f", q=2)[q]).then_inc(s_ffw, 16)
                sp.dma_start(w3[q * D:(q + 1) * D, :, q * D:(q + 1) * D], e_w3.rearrange("(j q) h f -> q h j f", q=2)[q]).then_inc(s_ffw, 16)
            sp.dma_start(b2[:], e_b2).then_inc(s_ffw, 16)
            sp.dma_start(wr2[0:RH, 0:NE], r_w2).then_inc(s_ffw, 16)
            sp.dma_start(wr2[RH:RH + 1, 0:NE], r_b2.rearrange("(a n) -> a n", a=1)).then_inc(s_ffw, 16)
            out_c = out.rearrange("b (c t) d -> c t b d", t=STEPS)
            with sp.Fori(0, NCH) as c:
                sp.wait_ge(f_comb, c * NE + NE)
                sp.dma_start(out_c[bass.ds(c, 1), :, :, :].rearrange("c t b d -> (c t) b d"), yout[:]).then_inc(s_out, 16)
            sp.wait_ge(s_out, 16 * NCH)

        @block.gpsimd
        def _(pool):
            nc.gpsimd.memset(w1[:], 0.0).then_inc(s_const, 1)
            nc.gpsimd.memset(w2[:], 0.0).then_inc(s_const, 1)
            nc.gpsimd.memset(w3[:], 0.0).then_inc(s_const, 1)
            nc.gpsimd.memset(wr2[:], 0.0).then_inc(s_const, 1)
            nc.gpsimd.memset(brow[:], 0.0).then_inc(s_const, 1)
            nc.gpsimd.memset(bpart[:], 0.0).then_inc(s_const, 1)
            pool.wait_ge(s_idx, 3)
            for c in range(2):
                nc.gpsimd.indirect_dma_start(rows[:, c, :], None, table, bass.IndirectOffsetOnAxis(ap=idx[:, c:c + 1], axis=0)).then_inc(s_rows[c], 16)
            nc.gpsimd.memset(ident[:], 0.0).then_inc(s_const, 1)
            pool.wait_ge(s_const, 7)
            nc.gpsimd.affine_select(out=ident[:], in_=ident[:], compare_op=ALU.not_equal, fill=1.0, base=0,
                                    pattern=[[-1, P]], channel_multiplier=1).then_inc(s_const, 1)
            nc.gpsimd.memset(ones[:], 1.0).then_inc(s_const, 1)
            nc.gpsimd.memset(fx[:], 0.0).then_inc(s_const, 1)
            nc.gpsimd.memset(xT[:, 0:P], 0.0).then_inc(s_const, 1)
            nc.gpsimd.memset(xT[:, (NCH + 1) * P:], 0.0).then_inc(s_const, 1)
            nc.gpsimd.memset(halfneg[:], -0.5).then_inc(s_const, 1)
            nc.gpsimd.iota(iota[:], [[1, NPAD]], channel_multiplier=0, allow_small_or_imprecise_dtypes=True).then_inc(s_const, 1)
            pool.wait_ge(s_const, 14)
            nc.gpsimd.memset(fx[:, D:D + 1], 1.0).then_inc(s_const, 1)
            nc.gpsimd.tensor_copy(ident16[:], ident[:]).then_inc(s_const, 1)
            pool.wait_ge(s_const, 16)
            nc.gpsimd.memset(w1[D:D + 1, PAIRS, RH:RH + 1], 1.0).then_inc(s_const, 1)
            pool.wait_ge(s_const, 17)
            nc.gpsimd.memset(wr2[RH:RH + 1, NE:NPAD], LEAST).then_inc(s_const, 1)
            for c in range(NCH):
                pool.wait_ge(s_ve, c + 1)
                nc.gpsimd.tensor_tensor(rstd[:], ve[:], halfneg[:], ALU.pow).then_inc(s_rstd, 1)
                if c + 2 < NCH:
                    pool.wait_ge(s_tr, c + 1)
                    nc.gpsimd.indirect_dma_start(rows[:, c % 2, :], None, table, bass.IndirectOffsetOnAxis(ap=idx[:, c + 2:c + 3], axis=0)).then_inc(s_rows[c % 2], 16)

            def ffn(i):
                pool.wait_ge(f_ve, i + 1)
                nc.gpsimd.tensor_tensor(rstd[:], ve[:], halfneg[:], ALU.pow).then_inc(f_rstd, 1)

            with pool.Fori(0, NCH) as i:
                ffn(i)

        def act_step(d, slot, k, zi_, zo_, ai_, ao_, at_, dc_, n):
            a = nc.scalar
            a.wait_ge(zi_, n)
            a.activation(gates[d][:, slot, 0:3 * B], z_ifg[d][:, k * 3 * B:(k + 1) * 3 * B], ACT.Tanh, scale=1 / S).then_inc(ai_, 1)
            a.wait_ge(zo_, n)
            a.activation(tho[d][:], z_o[d][:, k * B:(k + 1) * B], ACT.Tanh, scale=1 / S).then_inc(ao_, 1)

        def act_cell(d, slot, at_, dc_, n):
            nc.scalar.wait_ge(dc_, n)
            nc.scalar.activation(tc[d][:], gates[d][:, 1 - slot, 3 * B:4 * B], ACT.Tanh, scale=0.5).then_inc(at_, 1)

        @block.scalar
        def _(act):
            act.wait_ge(s_prep, 1)
            nc.scalar.activation(tc[0][:], h32[0][:], ACT.Tanh)
            with act.Fori(0, NCH) as c:
                act.wait_ge(s_tr, c + 1)
                nc.scalar.activation(rowsT[0:D, 4 * P:5 * P], pB[0:D, 0:P], ACT.Copy).then_inc(s_trB, 1)
                act.wait_ge(s_xnT, c + 1)
                nc.scalar.activation(xT[:, bass.ds(c * P + P, P)], pD[:, 0:P // 2].bitcast(F16), ACT.Copy).then_inc(s_xT, 1)
            with act.Fori(0, T, STEPS) as i:
                for s in range(STEPS):
                    for d in range(2):
                        k = s % SEED if d == 0 else SEED - 1 - s % SEED
                        act_step(d, s % 2, k, zi[d], zo[d], ai[d], ao[d], at[d], dc[d], i + s + 1)
                        act_cell(d, s % 2, at[d], dc[d], i + s + 1)

            def relu1(i, j):
                if j == PAIRS:
                    act.wait_ge(f_l1, i + 1)
                nc.scalar.activation(g1[:, j, :], pB[:, j * P:(j + 1) * P], ACT.Relu).then_inc(f_g1, 1)

            def relu2(i, j):
                if j == 0:
                    act.wait_ge(f_l2, i + 1)
                nc.scalar.activation(g2[:, j, :], pC[:, j * P:(j + 1) * P], ACT.Relu, bias=b2[:, j:j + 1]).then_inc(f_g2, 1)

            def chunk(i, steps, first, second):
                for s in range(STEPS):
                    if steps:
                        act_step(0, s % 2, s % SEED, dzi, dzo, dai, dao, dat, ddc, i * STEPS + s + 1)
                    if second and s == 1:
                        act.wait_ge(f_route[7], i - 1)
                        nc.scalar.activation(pe_[:], pd[:], ACT.Exp).then_inc(f_pe, 1)
                    if first and s == 6:
                        act.wait_ge(f_route[1], i)
                        nc.scalar.activation(ex[:], dl[:], ACT.Exp, accum_out=exs[:]).then_inc(f_ex, 1)
                    if steps:
                        act_cell(0, s % 2, dat, ddc, i * STEPS + s + 1)
                    if first:
                        if s == 2:
                            act.wait_ge(f_tr, i)
                            nc.scalar.activation(fxT[:], pA[:, P:2 * P], ACT.Copy).then_inc(f_fxT, 1)
                        if s == 4:
                            relu1(i - 1, PAIRS)
                            relu1(i - 1, 0)
                        if s == 5:
                            relu1(i - 1, 1)
                            relu1(i - 1, 2)
                        if s == 6:
                            relu2(i - 1, 0)
                            relu2(i - 1, 1)
                        if s == 7:
                            relu2(i - 1, 2)

            chunk(0, True, False, False)
            chunk(1, True, True, False)
            chunk(2, True, True, True)
            with act.Fori(3, NCH) as i:
                chunk(i, True, True, True)
            chunk(NCH, False, True, True)
            chunk(NCH + 1, False, False, True)

        def mm(o, l, r, start=False):
            return nc.tensor.matmul(o, l, r, start=start, stop=True, skip_group_check=True)

        def z_of(d, g, k, n=1):
            if g < 3:
                v = z_ifg[d][:, 0:SEED * 3 * B].rearrange("p (k c) -> p k c", c=3 * B)
                return v[:, k:k + n, g * B:(g + 1) * B]
            return z_o[d][:, k * B:(k + n) * B].rearrange("p (k c) -> p k c", c=B)

        def recur(d, uj, k, prev, zi_, zo_, dhi_, dlo_, n):
            gate = [slice(g * H, (g + 1) * H) for g in range(4)]
            nc.tensor.wait_ge(dhi_, n)
            for g in range(4):
                mm(z_of(d, g, k), hi[:, uj, gate[g]], hhi[d][:, prev, :])
                mm(z_of(d, g, k), lo[:, uj, gate[g]], hhi[d][:, prev, :])
            nc.tensor.wait_ge(dlo_, n)
            for g in range(4):
                last = mm(z_of(d, g, k), hi[:, uj, gate[g]], hlo[d][:, prev, :])
                if g == 2:
                    last.then_inc(zi_, 1)
                if g == 3:
                    last.then_inc(zo_, 1)

        def seed_input(d, col, waits):
            x = xT[:, bass.ds(col, SEED * B)]
            for g in range(4):
                if g == 0 and waits is not None:
                    nc.tensor.wait_ge(ai[d], waits)
                if g == 3 and waits is not None:
                    nc.tensor.wait_ge(ao[d], waits)
                cols = slice(g * H, (g + 1) * H)
                mm(z_of(d, g, 0, SEED), bpart[:, ENC_B[d], cols], ones[:, 0:SEED * B], start=g in (0, 3))
                mm(z_of(d, g, 0, SEED), hi[:, WF + d, cols], x)
                mm(z_of(d, g, 0, SEED), lo[:, WF + d, cols], x)

        def seed_const(waits):
            ifg = z_ifg[0][:, 0:SEED * 3 * B].rearrange("p (k c) -> p k c", c=3 * B)
            o = z_o[0][:, 0:SEED * B].rearrange("p (k c) -> p k c", c=B)
            if waits is not None:
                nc.tensor.wait_ge(dai, waits)
            mm(ifg, ident16[:], zc_hi[:, :, 0:3 * B], start=True)
            mm(ifg, ident16[:], zc_lo[:, :, 0:3 * B])
            if waits is not None:
                nc.tensor.wait_ge(dao, waits)
            mm(o, ident16[:], zc_hi[:, :, 3 * B:4 * B], start=True)
            mm(o, ident16[:], zc_lo[:, :, 3 * B:4 * B])

        @block.tensor
        def _(pe):
            pe.wait_ge(s_const, 18)
            pe.wait_ge(s_conv, 64)

            def embed(c, k):
                last_k = GK - (NK - 1) * P
                for m in range(NK - 1):
                    nc.tensor.transpose(pA[:, m * P:(m + 1) * P], rows[:, k, m * P:(m + 1) * P], ident[:])
                nc.tensor.transpose(pB[0:last_k, 0:P], rows[:, k, (NK - 1) * P:GK], ident[:]).then_inc(s_tr, 1)

            def embed_conv(c):
                last_k = GK - (NK - 1) * P
                pe.wait_ge(s_trA, c + 1)
                pe.wait_ge(s_trB, c + 1)
                for m in range(NK - 1):
                    mm(pC[:, 0:D], rowsT[:, m * P:(m + 1) * P], convw[:, m, :], start=m == 0)
                mm(pC[:, 0:D], rowsT[0:last_k, 4 * P:5 * P], convw[0:last_k, NK - 1, :]).then_inc(s_conv_mm, 1)
                pe.wait_ge(s_xn, 2 * c + 2)
                nc.tensor.transpose(pD[:, 0:P // 2].bitcast(F16), xn[:], ident16[:]).then_inc(s_xnT, 1)

            for c in range(2):
                pe.wait_ge(s_rows[c], 16)
                if c:
                    pe.wait_ge(s_trA, c)
                    pe.wait_ge(s_trB, c)
                embed(c, c)
                if c == 0:
                    embed_conv(c)
            with pe.Fori(2, NCH, 2) as c:
                for k in range(2):
                    embed_conv(c + k - 1)
                    pe.wait_ge(s_rows[k], c * 8 + 16)
                    embed(c + k, k)
            embed_conv(NCH - 1)

            pe.wait_ge(s_prep, PREP)
            pe.wait_ge(s_xT, NCH)
            seed_input(0, P, None)
            seed_input(1, NCH * P + SEED * B, None)
            with pe.Fori(0, NCH) as i:
                for s in range(STEPS):
                    for d in range(2):
                        k = s % SEED if d == 0 else SEED - 1 - s % SEED
                        n = i * STEPS + s + 1
                        recur(d, UF + d, k, (s - 1) % STEPS, zi[d], zo[d], dhi[d], dlo[d], n)
                        if s % SEED == SEED - 1:
                            if d == 0:
                                col = i * P + (P + (s + 1) * B)
                            else:
                                col = (NCH - i) * P - (s + 1 - SEED) * B
                            seed_input(d, col, n)
            for d in range(2):
                pe.wait_ge(dhi[d], T + 1)
                pe.wait_ge(dlo[d], T + 1)
            for g in range(4):
                cols = slice(g * H, (g + 1) * H)
                o = pA[:, g * B:(g + 1) * B]
                mm(o, bpart[:, DEC_B, cols], ones[:, 0:B], start=g == 0)
                for d in range(2):
                    mm(o, hi[:, WDF + d, cols], hhi[d][:, STEPS - 1, :])
                    mm(o, lo[:, WDF + d, cols], hhi[d][:, STEPS - 1, :])
                    last = mm(o, hi[:, WDF + d, cols], hlo[d][:, STEPS - 1, :])
            last.then_inc(s_zc, 1)
            pe.wait_ge(s_zcs, 3)
            seed_const(None)

            def l1(i, j):
                if j == PAIRS:
                    pe.wait_ge(f_fxT, i + 1)
                m = mm(pB[:, j * P:(j + 1) * P], w1[:, j, :], fxT[:], start=True)
                if j == PAIRS - 1:
                    m.then_inc(f_l1, 1)

            def chunk(i, steps, first, second):
                for s in range(STEPS):
                    if steps:
                        n = i * STEPS + s + 1
                        recur(0, UD, s % SEED, (s - 1) % STEPS, dzi, dzo, ddhi, ddlo, n)
                        if s % SEED == SEED - 1:
                            seed_const(n)
                    if first:
                        if s == 0:
                            if not steps:
                                pe.wait_ge(ddlo, i * STEPS + 1)
                            h_hi = hhi[0][:].rearrange("p s b -> p (s b)")
                            h_lo = hlo[0][:].rearrange("p s b -> p (s b)")
                            mm(pA[:, 0:D], h_hi, hi[:, WO, 0:D], start=True)
                            mm(pA[:, 0:D], h_hi, lo[:, WO, 0:D])
                            mm(pA[:, 0:D], h_lo, hi[:, WO, 0:D]).then_inc(f_proj, 1)
                        if s == 2:
                            pe.wait_ge(f_fx, i)
                            nc.tensor.transpose(pA[:, P:2 * P], fx[:], ident[:]).then_inc(f_tr, 1)
                        if s == 3:
                            l1(i - 1, PAIRS)
                            l1(i - 1, 0)
                        if s == 4:
                            l1(i - 1, 1)
                            l1(i - 1, 2)
                        if s == 5:
                            pe.wait_ge(f_g1, (i - 1) * 4 + 1)
                            mm(pA[:, 3 * P:3 * P + NPAD], g1[:, PAIRS, :], wr2[:], start=True).then_inc(f_lg, 1)
                            pe.wait_ge(f_g1, (i - 1) * 4 + 2)
                            mm(pC[:, 0:P], w2[:, 0, :], g1[:, 0, :], start=True)
                        if s == 6:
                            pe.wait_ge(f_g1, (i - 1) * 4 + 4)
                            mm(pC[:, P:2 * P], w2[:, 1, :], g1[:, 1, :], start=True)
                            mm(pC[:, 2 * P:3 * P], w2[:, 2, :], g1[:, 2, :], start=True).then_inc(f_l2, 1)
                    if second:
                        if s == 0:
                            if not (isinstance(i, int) and i == 2):
                                pe.wait_ge(f_comb, (i - 2) * NE)
                            mm(pD[:, 0:NE * D], ones[:], bpart[:, E3_B, 0:NE * D], start=True)
                            pe.wait_ge(f_g2, (i - 2) * 3 + 3)
                            mm(pD[:, 0:P], g2[:, 0, :], w3[:, 0, :])
                        if s == 1:
                            mm(pD[:, P:2 * P], g2[:, 1, :], w3[:, 1, :])
                            mm(pD[:, 2 * P:3 * P], g2[:, 2, :], w3[:, 2, :]).then_inc(f_l3, 1)

            pe.wait_ge(s_ffw, FFW)
            chunk(0, True, False, False)
            chunk(1, True, True, False)
            chunk(2, True, True, True)
            with pe.Fori(3, NCH) as i:
                chunk(i, True, True, True)
            chunk(NCH, False, True, True)
            chunk(NCH + 1, False, False, True)

        @block.vector
        def _(dve):
            v = nc.vector
            done = [0]

            def prep(ins, chain=True):
                done[0] += 1
                ins.then_inc(s_prep, 1)
                if chain:
                    dve.wait_ge(s_prep, done[0])

            def wait_apart(count, n):
                dve.wait_ge(s_ids, 16)
                dve.wait_ge(count, n)

            dve.wait_ge(s_ids, 16)
            v.tensor_scalar(idx_f[:], idx_in[:], float(-HALF), float(VOCAB - 1 + HALF), ALU.max, ALU.min).then_inc(s_idx, 1)
            dve.wait_ge(s_idx, 1)
            v.tensor_scalar(idx_f[:], idx_f[:], float(PAD - HALF), None, ALU.add).then_inc(s_idx, 1)
            dve.wait_ge(s_idx, 2)
            v.tensor_copy(idx[:], idx_f[:]).then_inc(s_idx, 1)
            for d in range(2):
                prep(v.memset(h32[d][:], 0.0), False)
                prep(v.memset(gates[d][:], 0.0), False)
                if d == 0:
                    v.memset(hlo[d][:], 0.0).then_inc(dlo[d], 1)
                v.memset(hhi[d][:], 0.0).then_inc(dhi[d], 1)
            dve.wait_ge(s_conv, 64)
            prep(v.tensor_tensor(cb[:], convb[:], bob[:], ALU.add))

            def embed_copy(c):
                dve.wait_ge(s_tr, c + 1)
                v.tensor_copy(rowsT[:, 0:4 * P], pA[:]).then_inc(s_trA, 1)

            def embed_norm(n):
                c = n - 1
                dve.wait_ge(s_conv_mm, c + 1)
                v.tensor_tensor(hx[:, 0, :], pC[:, 0:D], convb[:], ALU.add).then_inc(s_h1, 1)
                dve.wait_ge(s_h1, 2 * c + 1)
                v.tensor_tensor(h1[:, bass.ds(c, 1), :].rearrange("p c d -> p (c d)"), hx[:, 0, :], bob[:], ALU.add).then_inc(s_h1, 1)
                v.bn_stats(st[:], hx[:, 0, :]).then_inc(s_st, 1)
                wait_apart(s_st, n)
                v.bn_aggr(mv[:], st[:]).then_inc(s_mv, 1)
                dve.wait_ge(s_mv, n)
                v.tensor_scalar(ve[:], mv[:, 1:2], EPS, None, ALU.add).then_inc(s_ve, 1)
                dve.wait_ge(s_rstd, c + 1)
                v.tensor_scalar(xn[:, 0:D], hx[:, 0, :], mv[:, 0:1], rstd[:], ALU.subtract, ALU.mult).then_inc(s_xn, 1)
                v.tensor_scalar(xn32[:], hx[:, 0, :], mv[:, 0:1], rstd[:], ALU.subtract, ALU.mult).then_inc(s_xn32, 1)
                dve.wait_ge(s_xn32, c + 1)
                dve.wait_ge(s_xn, 2 * c + 1)
                v.tensor_tensor(xn[:, D:2 * D], xn32[:], xn[:, 0:D], ALU.subtract).then_inc(s_xn, 1)

            with dve.Fori(1, NCH + 1) as n:
                embed_copy(n - 1)
                embed_norm(n)

            dve.wait_ge(s_lstm, 16 * 10)
            for j in range(8):
                n = D if j == WO else 4 * H
                prep(v.tensor_scalar(raw[:, j, 0:n], raw[:, j, 0:n], FACT[j], None, ALU.mult))
                if j != WO:
                    prep(v.tensor_scalar(raw[:, j, G], raw[:, j, G], 2.0, None, ALU.mult))
                prep(v.tensor_copy(hi[:, j, 0:n], raw[:, j, 0:n]))
                prep(v.tensor_tensor(lo[:, j, 0:n], raw[:, j, 0:n], hi[:, j, 0:n], ALU.subtract))
            dve.wait_ge(s_small, 16 * 12)
            dve.wait_ge(s_const, 6)
            prep(v.tensor_scalar(brow[:, 0:3, :], brow[:, 0:3, :], S / 2, None, ALU.mult))
            prep(v.tensor_scalar(brow[:, 0:3, G], brow[:, 0:3, G], 2.0, None, ALU.mult))
            prep(v.tensor_copy(bp_hi[:], brow[:]))
            prep(v.tensor_tensor(brest[:], brow[:], bp_hi[:], ALU.subtract))
            prep(v.tensor_copy(bp_mid[:], brest[:]))
            prep(v.tensor_copy(bpart[0:1, :, :], bp_hi[0:1, :, :]), False)
            prep(v.tensor_copy(bpart[32:33, :, :], bp_mid[32:33, :, :]), False)
            prep(v.tensor_tensor(bpart[64:65, :, :], brest[64:65, :, :], bp_mid[64:65, :, :], ALU.subtract), True)
            assert done[0] == PREP, done[0]

            def products(d, slot, ai_, dp_, n):
                dve.wait_ge(ai_, n)
                v.scalar_tensor_tensor(out=prod[d][:], in0=gates[d][:, slot, 0:2 * B], scalar=1.0,
                                       in1=gates[d][:, slot, 2 * B:4 * B], op0=ALU.add, op1=ALU.mult).then_inc(dp_, 1)

            def cell(d, slot, dp_, dc_, n):
                dve.wait_ge(dp_, n)
                v.scalar_tensor_tensor(out=gates[d][:, 1 - slot, 3 * B:4 * B], in0=prod[d][:, B:2 * B], scalar=0.5,
                                       in1=prod[d][:, 0:B], op0=ALU.mult, op1=ALU.add).then_inc(dc_, 1)

            def hidden(d, s, ao_, at_, dhi_, dh_, n):
                dve.wait_ge(ao_, n)
                dve.wait_ge(at_, n)
                v.scalar_tensor_tensor(out=hhi[d][:, s, :], in0=tho[d][:], scalar=1.0, in1=tc[d][:],
                                       op0=ALU.add, op1=ALU.mult).then_inc(dhi_, 1)
                v.scalar_tensor_tensor(out=h32[d][:], in0=tho[d][:], scalar=1.0, in1=tc[d][:],
                                       op0=ALU.add, op1=ALU.mult).then_inc(dh_, 1)

            def low(d, s, dhi_, dh_, dlo_, n):
                if n is not None:
                    dve.wait_ge(dh_, n)
                    dve.wait_ge(dhi_, n + 1)
                v.tensor_tensor(hlo[d][:, s, :], h32[d][:], hhi[d][:, s, :], ALU.subtract).then_inc(dlo_, 1)

            low(1, STEPS - 1, None, None, dlo[1], None)

            with dve.Fori(0, T, STEPS) as i:
                for s in range(STEPS):
                    n = i + s + 1
                    products(0, s % 2, ai[0], dp[0], n)
                    cell(0, s % 2, dp[0], dc[0], n)
                    hidden(0, s, ao[0], at[0], dhi[0], dh[0], n)
                    products(1, s % 2, ai[1], dp[1], n)
                    low(0, s, dhi[0], dh[0], dlo[0], n)
                    cell(1, s % 2, dp[1], dc[1], n)
                    hidden(1, s, ao[1], at[1], dhi[1], dh[1], n)
                    low(1, s, dhi[1], dh[1], dlo[1], n)

            dve.wait_ge(s_zc, 1)
            v.tensor_copy(zc32[:], pA[:, 0:4 * B]).then_inc(s_zcs, 1)
            dve.wait_ge(s_zcs, 1)
            zc_b = zc32[:].rearrange("p (a c) -> p a c", a=1).broadcast_to([P, SEED, 4 * B])
            v.tensor_copy(zc_hi[:], zc_b).then_inc(s_zcs, 1)
            dve.wait_ge(s_zcs, 2)
            v.memset(gates[0][:], 0.0).then_inc(s_prep, 1)
            v.memset(hlo[0][:], 0.0).then_inc(ddlo, 1)
            v.memset(hhi[0][:], 0.0).then_inc(ddhi, 1)
            v.tensor_tensor(zc_lo[:], zc_b, zc_hi[:], ALU.subtract).then_inc(s_zcs, 1)
            dve.wait_ge(s_prep, PREP + 1)

            def route(n, k, apart=False):
                (wait_apart if apart else dve.wait_ge)(f_route[k - 2], n)

            def chunk(i, steps, first, second):
                for s in range(STEPS):
                    n = i * STEPS + s + 1
                    if steps:
                        products(0, s % 2, dai, ddp, n)
                        cell(0, s % 2, ddp, ddc, n)
                    a, b = i - 1, i - 2
                    if second:
                        if s == 1:
                            dve.wait_ge(f_pe, b + 1)
                            v.tensor_scalar(pden[:], pe_[:], 1.0, None, ALU.add).then_inc(f_route[8], 1)
                        if 3 <= s < 6:
                            comb(b, 2 * (s - 3))
                    if steps:
                        if s == 0 and first:
                            dve.wait_ge(f_proj, i)
                        hidden(0, s, dao, dat, ddhi, ddh, n)
                        low(0, s, ddhi, ddh, ddlo, n)
                    if first:
                        if s == 0:
                            dve.wait_ge(f_proj, i)
                            if second:
                                dve.wait_ge(f_yres, i - 1)
                            v.scalar_tensor_tensor(out=y1[:], in0=pA[:, 0:D], scalar=1 / S,
                                                   in1=h1[:, bass.ds(a, 1), :].rearrange("p c d -> p (c d)"),
                                                   op0=ALU.mult, op1=ALU.add).then_inc(f_y1, 1)
                            dve.wait_ge(f_y1, i)
                            v.bn_stats(st[:], y1[:]).then_inc(f_st, 1)
                            wait_apart(f_st, i)
                            v.bn_aggr(mv[:], st[:]).then_inc(f_mv, 1)
                        if s == 1:
                            dve.wait_ge(f_mv, i)
                            v.tensor_scalar(ve[:], mv[:, 1:2], EPS, None, ALU.add).then_inc(f_ve, 1)
                        if s == 2:
                            dve.wait_ge(f_rstd, i)
                            v.tensor_scalar(fx[:, 0:D], y1[:], mv[:, 0:1], rstd[:], ALU.subtract, ALU.mult).then_inc(f_fx, 1)
                    if second:
                        if s == 1:
                            route(i - 1, 10)
                            v.reciprocal(wt0[:], pden[:]).then_inc(f_route[9], 1)
                            route(i - 1, 11)
                            v.tensor_scalar(rw0[:], iota[:], topf[:, 0:1], wt0[:], ALU.is_equal, ALU.mult).then_inc(f_route[10], 1)
                        if s == 2:
                            route(i - 1, 12)
                            v.tensor_tensor(wt1[:], pe_[:], wt0[:], ALU.mult).then_inc(f_route[11], 1)
                            route(i - 1, 13)
                            v.tensor_scalar(rw1[:], iota[:], topf[:, 1:2], wt1[:], ALU.is_equal, ALU.mult).then_inc(f_route[12], 1)
                            route(i - 1, 14)
                            v.tensor_tensor(rw[:], rw0[:], rw1[:], ALU.add).then_inc(f_route[13], 1)
                        if 3 <= s < 6:
                            comb(b, 2 * (s - 3) + 1)
                    if first:
                        if s == 5:
                            wait_apart(f_lg, i)
                            v.max(m8[:], pA[:, 3 * P:3 * P + NPAD]).then_inc(f_route[0], 1)
                            route(i, 2)
                            v.tensor_scalar(dl[:], pA[:, 3 * P:3 * P + NPAD], m8[:, 0:1], None, ALU.subtract).then_inc(f_route[1], 1)
                        if s == 6:
                            dve.wait_ge(f_ex, i)
                            v.reciprocal(exr[:], exs[:]).then_inc(f_route[2], 1)
                            route(i, 4)
                            v.tensor_scalar(pr[:], ex[:], exr[:], None, ALU.mult).then_inc(f_route[3], 1)
                            route(i, 5, apart=True)
                            v.max(p8[:], pr[:]).then_inc(f_route[4], 1)
                        if s == 7:
                            route(i, 6, apart=True)
                            v.max_index(top[:], p8[:], pr[:]).then_inc(f_route[5], 1)
                            route(i, 7)
                            v.tensor_copy(topf[:], top[:]).then_inc(f_route[6], 1)
                            v.tensor_tensor(pd[:], p8[:, 1:2], p8[:, 0:1], ALU.subtract).then_inc(f_route[7], 1)
                            v.tensor_copy(yres[:], y1[:]).then_inc(f_yres, 1)

            def comb(b, e):
                if e == 0:
                    dve.wait_ge(f_l3, b + 1)
                    dve.wait_ge(f_route[ROUTE - 1], b + 1)
                    dve.wait_ge(f_yres, b + 1)
                else:
                    dve.wait_ge(f_comb, b * NE + e)
                if e == NE - 1 and not (isinstance(b, int) and b == 0):
                    dve.wait_ge(s_out, 16 * b)
                v.scalar_tensor_tensor(out=yout[:] if e == NE - 1 else acc[:], in0=pD[:, e * D:(e + 1) * D],
                                       scalar=rw[:, e:e + 1], in1=yres[:] if e == 0 else acc[:],
                                       op0=ALU.mult, op1=ALU.add).then_inc(f_comb, 1)

            chunk(0, True, False, False)
            chunk(1, True, True, False)
            chunk(2, True, True, True)
            with dve.Fori(3, NCH) as i:
                chunk(i, True, True, True)
            chunk(NCH, False, True, True)
            chunk(NCH + 1, False, False, True)


ROUTE = 14
PREP = 4 + 1 + 7 * 4 + 3 + 8

_IN = ["L0_tok_b", "L0_attn_Wf", "L0_attn_Uf", "L0_attn_bf", "L0_attn_Wb", "L0_attn_Ub", "L0_attn_bb",
       "L0_attn_Wd", "L0_attn_Ud", "L0_attn_bd", "L0_attn_Wo", "L0_attn_bo", "L0_ffn_router_w1",
       "L0_ffn_router_b1", "L0_ffn_router_w2", "L0_ffn_router_b2", "L0_ffn_expert_w1", "L0_ffn_expert_b1",
       "L0_ffn_expert_w2", "L0_ffn_expert_b2", "L0_ffn_expert_w3", "L0_ffn_expert_b3"]


def kernel(**inputs):
    import numpy as np
    import concourse.bacc as bacc
    from concourse.bass_utils import run_bass_kernel_spmd as run

    nc = bacc.Bacc("TRN2", target_bir_lowering=False, num_devices=1)
    a = {k: np.ascontiguousarray(inputs[k]) for k in _IN}
    a["ids"] = np.ascontiguousarray(np.asarray(inputs["x"]).reshape(B, NCH, STEPS).transpose(2, 0, 1).reshape(P, NCH))
    emb = np.asarray(inputs["L0_tok_emb"])
    a["table"] = np.concatenate([np.repeat(emb[:1], PAD, axis=0), emb, np.repeat(emb[-1:], PAD, axis=0)])
    a["L0_ffn_expert_b2"] = np.ascontiguousarray(a["L0_ffn_expert_b2"].reshape(PAIRS, P).T)
    a["conv_w"] = np.ascontiguousarray(np.asarray(inputs["L0_tok_W"]).transpose(2, 1, 0))
    t = {k: nc.dram_tensor("in_" + k, x.shape, mybir.dt.from_np(x.dtype), kind="ExternalInput").ap() for k, x in a.items()}
    o = nc.dram_tensor("out_h", (B, T, D), F32, kind="ExternalOutput").ap()
    at = lambda n: t["L0_attn_" + n]
    ff = lambda n: t["L0_ffn_" + n]
    tower(nc, t["ids"], t["table"], t["conv_w"], t["L0_tok_b"], (at("Wf"), at("Wb")), (at("Uf"), at("Ub")),
          (at("bf"), at("bb")), at("Wd"), at("Ud"), at("bd"), at("Wo"), at("bo"),
          ff("router_w1"), ff("router_b1"), ff("router_w2"), ff("router_b2"), ff("expert_w1"), ff("expert_b1"),
          ff("expert_w2"), ff("expert_b2"), ff("expert_w3"), ff("expert_b3"), o)
    r = run(nc, [{"in_" + k: x for k, x in a.items()}], core_ids=[0])
    return r.results[0]["out_h"]
```

```python
from contextlib import ExitStack

import concourse.bass as bass
from concourse import mybir

F32 = mybir.dt.float32
F16 = mybir.dt.float16
BF16 = mybir.dt.bfloat16
I32 = mybir.dt.int32
U32 = mybir.dt.uint32
ALU = mybir.AluOpType
ACT = mybir.ActivationFunctionType

B, T = 16, 512
D = 64
KS = 9
H = 128
NE = 6
RH = 32
VOCAB = 50257
HALF = KS // 2
PAD = 2 * HALF
P = 128
STEPS = P // B
NCH = T // STEPS
SEED = STEPS // 2
GK = KS * D
NK = (GK + P - 1) // P
PAIRS = NE // 2
NPAD = 8
EPS = 1e-5
S = 256.0
SX = 256.0
SW = 256.0
BODY = 4
LEAD = 6
LEAST = -1.0e30


def tower(nc, ids, table, conv_w, conv_b, w_in, u_in, b_in, wd, ud, bd, wo, bo,
          r_w1, r_b1, r_w2, r_b2, e_w1, e_b1, e_w2, e_b2, e_w3, e_b3, out):
    with ExitStack() as ctx:
        def sb(name, shape, dt=F32):
            return ctx.enter_context(nc.sbuf_tensor(name, shape, dt))

        def bank(name, dt=F32):
            return ctx.enter_context(nc.psum_tensor(name, [P, 2048 // (4 if dt == F32 else 2)], dt))

        def sem(name):
            return ctx.enter_context(nc.semaphore(name))

        raw = sb("raw", [P, 8, 4 * H])
        hi = sb("hi", [P, 8, 4 * H], F16)
        lo = sb("lo", [P, 8, 4 * H], F16)
        brow = sb("brow", [P, 4, 4 * H])
        brest = sb("brest", [P, 4, 4 * H])
        bp_hi = sb("bp_hi", [P, 4, 4 * H], BF16)
        bp_mid = sb("bp_mid", [P, 4, 4 * H], BF16)
        bpart = sb("bpart", [P, 4, 4 * H], BF16)
        ones = sb("ones", [P, P], BF16)
        ident = sb("ident", [P, P])
        ident16 = sb("ident16", [P, P], F16)
        convw = sb("convw", [P, NK, D])
        cw_hi = sb("cw_hi", [P, NK, D], F16)
        cw_lo = sb("cw_lo", [P, NK, D], F16)
        convb = sb("convb", [P, D])
        bob = sb("bob", [P, D])
        w1 = sb("w1", [P, PAIRS + 1, P])
        w2 = sb("w2", [P, PAIRS, P])
        b2 = sb("b2", [P, PAIRS])
        w3 = sb("w3", [P, PAIRS, P])
        wr2 = sb("wr2", [P, NPAD])
        iota = sb("iota", [P, NPAD])
        halfneg = sb("halfneg", [P, 1])
        idx_in = sb("idx_in", [P, NCH], I32)
        idx_f = sb("idx_f", [P, NCH])
        idx = sb("idx", [P, NCH], I32)
        rows = sb("rows", [P, 2, GK])
        idx_c = sb("idx_c", [P, 2], I32)
        rowsT = sb("rowsT", [P, NK * P])
        rT_hi = sb("rT_hi", [P, 2, NK * P], F16)
        rT_lo = sb("rT_lo", [P, NK * P], F16)
        h1 = sb("h1", [P, NCH, D])
        hx = sb("hx", [P, D])
        st = sb("st", [P, 6])
        mv = sb("mv", [P, 2])
        ve = sb("ve", [P, 1])
        rstd = sb("rstd", [P, 1])
        xn32 = sb("xn32", [P, D])
        xn = sb("xn", [P, 2 * D], F16)
        xT = sb("xT", [P, (NCH + 2) * P], F16)
        gates = [sb(f"gates{d}", [P, 2, 4 * B]) for d in "fb"]
        tho = [sb(f"tho{d}", [P, B]) for d in "fb"]
        prod = [sb(f"prod{d}", [P, 2 * B]) for d in "fb"]
        tc = [sb(f"tc{d}", [P, B]) for d in "fb"]
        h32 = [sb(f"h32{d}", [P, B]) for d in "fb"]
        hhi = [sb(f"hhi{d}", [P, STEPS, B], F16) for d in "fb"]
        hlo = [sb(f"hlo{d}", [P, STEPS, B], F16) for d in "fb"]
        zc32 = sb("zc32", [P, 4 * B])
        zc_hi = sb("zc_hi", [P, SEED, 4 * B], F16)
        zc_lo = sb("zc_lo", [P, SEED, 4 * B], F16)
        y1 = sb("y1", [P, D])
        yres = sb("yres", [P, D])
        acc = sb("acc", [P, D])
        yout = sb("yout", [P, D])
        fx = sb("fx", [P, P])
        fxT = sb("fxT", [P, P])
        g1 = sb("g1", [P, PAIRS + 1, P])
        g2 = sb("g2", [P, PAIRS, P])
        m8 = sb("m8", [P, NPAD])
        dl = sb("dl", [P, NPAD])
        ex = sb("ex", [P, NPAD])
        exs = sb("exs", [P, 1])
        exr = sb("exr", [P, 1])
        pr = sb("pr", [P, NPAD])
        p8 = sb("p8", [P, NPAD])
        top = sb("top", [P, NPAD], U32)
        topf = sb("topf", [P, NPAD])
        pd = sb("pd", [P, 1])
        pe_ = sb("pe_", [P, 1])
        pden = sb("pden", [P, 1])
        wt0 = sb("wt0", [P, 1])
        wt1 = sb("wt1", [P, 1])
        rw0 = sb("rw0", [P, NPAD])
        rw1 = sb("rw1", [P, NPAD])
        rw = sb("rw", [P, NPAD])

        z_ifg = [[bank(f"z_ifg_{d}{k}") for k in range(2)] for d in "fb"]
        z_o = [bank("z_o_f"), bank("z_o_b")]
        pA, pB = bank("pA"), bank("pB")
        pC, pD = z_ifg[1]

        s_ids = sem("s_ids")
        s_conv = sem("s_conv")
        s_small = sem("s_small")
        s_lstm = sem("s_lstm")
        s_ffw = sem("s_ffw")
        s_const = sem("s_const")
        s_idx = sem("s_idx")
        s_zero = sem("s_zero")
        s_scaled = sem("s_scaled")
        s_prep = sem("s_prep")
        s_rows = [sem("s_rows0"), sem("s_rows1")]
        s_cw = sem("s_cw")
        e_t4 = sem("e_t4")
        e_tr = sem("e_tr")
        e_r4 = sem("e_r4")
        e_evac = sem("e_evac")
        e_idx = sem("e_idx")
        e_split = sem("e_split")
        e_conv = sem("e_conv")
        e_hx = sem("e_hx")
        e_h1 = sem("e_h1")
        e_st = sem("e_st")
        e_mv = sem("e_mv")
        e_ve = sem("e_ve")
        e_rstd = sem("e_rstd")
        e_xn32 = sem("e_xn32")
        e_xn = sem("e_xn")
        e_xnT = sem("e_xnT")
        e_xT = sem("e_xT")
        s_prep2 = sem("s_prep2")
        zi = [sem("zi_f"), sem("zi_b")]
        zo = [sem("zo_f"), sem("zo_b")]
        ai = [sem("ai_f"), sem("ai_b")]
        ao = [sem("ao_f"), sem("ao_b")]
        at = [sem("at_f"), sem("at_b")]
        dp = [sem("dp_f"), sem("dp_b")]
        dc = [sem("dc_f"), sem("dc_b")]
        dhi = [sem("dhi_f"), sem("dhi_b")]
        dh = [sem("dh_f"), sem("dh_b")]
        dlo = [sem("dlo_f"), sem("dlo_b")]
        s_zc = sem("s_zc")
        s_zcs = sem("s_zcs")
        dzi, dzo, dai, dao, dat = sem("dzi"), sem("dzo"), sem("dai"), sem("dao"), sem("dat")
        ddp, ddc, ddhi, ddh, ddlo = sem("ddp"), sem("ddc"), sem("ddhi"), sem("ddh"), sem("ddlo")
        f_proj = sem("f_proj")
        f_y1 = sem("f_y1")
        f_st = sem("f_st")
        f_mv = sem("f_mv")
        f_ve = sem("f_ve")
        f_rstd = sem("f_rstd")
        f_fx = sem("f_fx")
        f_tr = sem("f_tr")
        f_fxT = sem("f_fxT")
        f_l1 = sem("f_l1")
        f_g1 = [sem(f"f_g1_{j}") for j in range(PAIRS + 1)]
        f_lg = sem("f_lg")
        f_l2 = sem("f_l2")
        f_g2 = [sem(f"f_g2_{j}") for j in range(PAIRS)]
        f_l3 = sem("f_l3")
        f_route = [sem(f"f_route{k}") for k in range(1, ROUTE + 1)]
        f_ex = sem("f_ex")
        f_pe = sem("f_pe")
        f_yres = sem("f_yres")
        f_comb = [sem(f"f_comb{e}") for e in range(NE)]
        s_out = sem("s_out")

        block = ctx.enter_context(nc.Block())

        UF, UB, UD, WF, WB, WDF, WDB, WO = range(8)
        FACT = {UF: S / 4, UB: S / 4, UD: S / 4, WF: S / 2, WB: S / 2, WDF: S / 4, WDB: S / 4, WO: S / 2}
        ENC_B, DEC_B, E3_B = (0, 1), 2, 3
        G = slice(2 * H, 3 * H)
        SMALL = 16 * 10
        FFW = 16 * 11

        @block.sync
        def _(sp):
            sp.dma_start(idx_in[:], ids).then_inc(s_ids, 16)
            cw = conv_w.rearrange("k h o -> (k h) o")
            sp.dma_start(convw[:, 0:NK - 1, :], cw[0:(NK - 1) * P, :].rearrange("(m p) o -> p m o", p=P)).then_inc(s_conv, 16)
            sp.dma_start(convw[0:GK - (NK - 1) * P, NK - 1, :], cw[(NK - 1) * P:GK, :]).then_inc(s_conv, 16)
            sp.dma_start(convb[:], conv_b.rearrange("(a d) -> a d", a=1).broadcast_to([P, D])).then_inc(s_conv, 16)
            sp.dma_start(bob[:], bo.rearrange("(a d) -> a d", a=1).broadcast_to([P, D])).then_inc(s_conv, 16)
            for j, w in ((UF, u_in[0]), (UB, u_in[1]), (UD, ud)):
                sp.dma_start(raw[:, j, :], w).then_inc(s_lstm, 16)
            for j, w in ((WF, w_in[0]), (WB, w_in[1])):
                for q in range(2):
                    sp.dma_start(raw[q * D:(q + 1) * D, j, :], w).then_inc(s_lstm, 16)
            sp.dma_start(raw[:, WDF, :], wd[0:H, :]).then_inc(s_lstm, 16)
            sp.dma_start(raw[:, WDB, :], wd[H:2 * H, :]).then_inc(s_lstm, 16)
            sp.dma_start(raw[:, WO, 0:D], wo).then_inc(s_lstm, 16)
            sp.wait_ge(s_zero, 2)
            for q in (0, 32, 64):
                for j, b in enumerate((b_in[0], b_in[1], bd)):
                    sp.dma_start(brow[q:q + 1, j, :], b.rearrange("(a n) -> a n", a=1)).then_inc(s_small, 16)
                sp.dma_start(brow[q:q + 1, E3_B, 0:NE * D], e_b3.rearrange("(a e) d -> a (e d)", a=1)).then_inc(s_small, 16)
            sp.wait_ge(s_const, 14)
            sp.dma_start(w1[0:D, 0:PAIRS, :].rearrange("p j (q h) -> p (j q) h", q=2), e_w1.rearrange("e d h -> d e h")).then_inc(s_ffw, 16)
            sp.dma_start(w1[D:D + 1, 0:PAIRS, :].rearrange("p j c -> p (j c)"), e_b1.rearrange("(a e) h -> a (e h)", a=1)).then_inc(s_ffw, 16)
            sp.dma_start(w1[0:D, PAIRS, 0:RH], r_w1).then_inc(s_ffw, 16)
            sp.dma_start(w1[D:D + 1, PAIRS, 0:RH], r_b1.rearrange("(a n) -> a n", a=1)).then_inc(s_ffw, 16)
            for q in range(2):
                sp.dma_start(w2[q * D:(q + 1) * D, :, q * D:(q + 1) * D], e_w2.rearrange("(j q) h f -> q h j f", q=2)[q]).then_inc(s_ffw, 16)
                sp.dma_start(w3[q * D:(q + 1) * D, :, q * D:(q + 1) * D], e_w3.rearrange("(j q) h f -> q h j f", q=2)[q]).then_inc(s_ffw, 16)
            sp.dma_start(b2[:], e_b2).then_inc(s_ffw, 16)
            sp.dma_start(wr2[0:RH, 0:NE], r_w2).then_inc(s_ffw, 16)
            sp.dma_start(wr2[RH:RH + 1, 0:NE], r_b2.rearrange("(a n) -> a n", a=1)).then_inc(s_ffw, 16)
            out_c = out.rearrange("b (c t) d -> c t b d", t=STEPS)
            with sp.Fori(0, NCH) as c:
                sp.wait_ge(f_comb[NE - 1], c + 1)
                sp.dma_start(out_c[bass.ds(c, 1), :, :, :].rearrange("c t b d -> (c t) b d"), yout[:]).then_inc(s_out, 16)
            sp.wait_ge(s_out, 16 * NCH)

        @block.gpsimd
        def _(pool):
            pool.wait_ge(s_idx, 3)
            for c, col in enumerate((0, NCH - 1)):
                nc.gpsimd.indirect_dma_start(rows[:, c, :], None, table, bass.IndirectOffsetOnAxis(ap=idx[:, col:col + 1], axis=0)).then_inc(s_rows[c], 16)
            nc.gpsimd.memset(ident[:], 0.0).then_inc(s_const, 1)
            pool.wait_ge(s_const, 1)
            nc.gpsimd.affine_select(out=ident[:], in_=ident[:], compare_op=ALU.not_equal, fill=1.0, base=0,
                                    pattern=[[-1, P]], channel_multiplier=1).then_inc(s_const, 1)
            nc.gpsimd.memset(rowsT[:, (NK - 1) * P:NK * P], 0.0).then_inc(s_const, 1)
            nc.gpsimd.memset(rT_hi[:, :, (NK - 1) * P:NK * P], 0.0).then_inc(s_const, 1)
            nc.gpsimd.memset(halfneg[:], -0.5).then_inc(s_const, 1)
            pool.wait_ge(s_const, 2)
            nc.gpsimd.tensor_copy(ident16[:], ident[:]).then_inc(s_const, 1)
            nc.gpsimd.memset(xT[:, 0:P], 0.0).then_inc(s_const, 1)
            nc.gpsimd.memset(xT[:, (NCH + 1) * P:], 0.0).then_inc(s_const, 1)
            nc.gpsimd.memset(ones[:], 1.0).then_inc(s_const, 1)

            def wait_apart(count, n):
                pool.wait_ge(s_idx, 3)
                pool.wait_ge(count, n)

            def embed(j, i, q, t, c, n):
                if c:
                    pool.wait_ge(e_evac, SEED * (j + 6))
                    if not isinstance(j, int) or j > -5:
                        pool.wait_ge(e_conv, SEED * (j + 5))
                    nc.gpsimd.tensor_tensor(rT_lo[:], rowsT[:], rT_hi[:, 1 - q, :], ALU.subtract).then_inc(e_split, SEED)
                if n:
                    chunk = i + 2 if q == 0 else NCH - 3 - i
                    wait_apart(e_hx, SEED * (j + 5))
                    nc.gpsimd.tensor_tensor(h1[:, bass.ds(chunk, 1), :].rearrange("p c d -> p (c d)"), hx[:], bob[:], ALU.add).then_inc(e_h1, SEED)
                    if t:
                        pool.wait_ge(e_t4, SEED * (j + 7))
                    pool.wait_ge(e_ve, SEED * (j + 5))
                    nc.gpsimd.tensor_tensor(rstd[:], ve[:], halfneg[:], ALU.pow).then_inc(e_rstd, SEED)
                if t:
                    chunk = i + 4 if q == 0 else NCH - 5 - i
                    if not n:
                        pool.wait_ge(e_t4, SEED * (j + 7))
                    nc.gpsimd.tensor_copy(idx_c[:, q:q + 1], idx[:, bass.ds(chunk, 1)]).then_inc(e_idx, 1)
                    wait_apart(e_idx, j + LEAD + 1)
                    pool.wait_ge(e_tr, SEED * (j + 7))
                    nc.gpsimd.indirect_dma_start(rows[:, q, :], None, table, bass.IndirectOffsetOnAxis(ap=idx_c[:, q:q + 1], axis=0)).then_inc(s_rows[q], 16)

            def consts(k):
                if k == 0:
                    nc.gpsimd.memset(w1[:], 0.0).then_inc(s_const, 1)
                    nc.gpsimd.memset(wr2[:], 0.0).then_inc(s_const, 1)
                    nc.gpsimd.memset(fx[:], 0.0).then_inc(s_const, 1)
                if k == 1:
                    nc.gpsimd.memset(w2[:], 0.0).then_inc(s_const, 1)
                    nc.gpsimd.memset(w3[:], 0.0).then_inc(s_const, 1)
                if k == 2:
                    nc.gpsimd.iota(iota[:], [[1, NPAD]], channel_multiplier=0, allow_small_or_imprecise_dtypes=True).then_inc(s_const, 1)
                    pool.wait_ge(s_const, 15)
                    nc.gpsimd.memset(fx[:, D:D + 1], 1.0).then_inc(s_const, 1)
                    pool.wait_ge(s_const, 16)
                    nc.gpsimd.memset(w1[D:D + 1, PAIRS, RH:RH + 1], 1.0).then_inc(s_const, 1)
                    pool.wait_ge(s_const, 17)
                    nc.gpsimd.memset(wr2[RH:RH + 1, NE:NPAD], LEAST).then_inc(s_const, 1)
                    pool.wait_ge(s_const, 18)

            for j in range(-LEAD, 0):
                embed(j, j // 2, j % 2, True, j >= -5, j >= -4)
                consts(j + LEAD)
            with pool.Fori(0, NCH // 2 - 4) as i:
                for q in range(2):
                    embed(2 * i + q, i, q, True, True, True)
            for j in range(NCH - 8, NCH - 4):
                embed(j, j // 2, j % 2, False, j < NCH - 5, True)
            done = [0]

            def prep(ins):
                done[0] += 1
                ins.then_inc(s_prep2, 1)
                pool.wait_ge(s_prep2, done[0])

            g = nc.gpsimd
            pool.wait_ge(s_lstm, 16 * 10)
            for j in (UD, WDF, WDB, WO):
                n = D if j == WO else 4 * H
                prep(g.tensor_scalar(raw[:, j, 0:n], raw[:, j, 0:n], FACT[j], None, ALU.mult))
                if j != WO:
                    prep(g.tensor_scalar(raw[:, j, G], raw[:, j, G], 2.0, None, ALU.mult))
                prep(g.tensor_copy(hi[:, j, 0:n], raw[:, j, 0:n]))
                prep(g.tensor_tensor(lo[:, j, 0:n], raw[:, j, 0:n], hi[:, j, 0:n], ALU.subtract))
            pool.wait_ge(s_small, 16 * 12)
            pool.wait_ge(s_zero, 2)
            prep(g.tensor_scalar(brow[:, DEC_B, :], brow[:, DEC_B, :], S / 2, None, ALU.mult))
            prep(g.tensor_scalar(brow[:, DEC_B, G], brow[:, DEC_B, G], 2.0, None, ALU.mult))
            prep(g.tensor_copy(bp_hi[:, 2:4, :], brow[:, 2:4, :]))
            prep(g.tensor_tensor(brest[:, 2:4, :], brow[:, 2:4, :], bp_hi[:, 2:4, :], ALU.subtract))
            prep(g.tensor_copy(bp_mid[:, 2:4, :], brest[:, 2:4, :]))
            prep(g.tensor_copy(bpart[0:1, 2:4, :], bp_hi[0:1, 2:4, :]))
            prep(g.tensor_copy(bpart[32:33, 2:4, :], bp_mid[32:33, 2:4, :]))
            prep(g.tensor_tensor(bpart[64:65, 2:4, :], brest[64:65, 2:4, :], bp_mid[64:65, 2:4, :], ALU.subtract))
            assert done[0] == PREP2, done[0]

            def ffn(i):
                pool.wait_ge(f_ve, i + 1)
                nc.gpsimd.tensor_tensor(rstd[:], ve[:], halfneg[:], ALU.pow).then_inc(f_rstd, 1)

            with pool.Fori(0, NCH) as i:
                ffn(i)

        def place(d, s):
            return s % SEED if d == 0 else SEED - 1 - s % SEED

        def act_step(d, s, zi_, zo_, ai_, ao_, at_, dc_, n):
            a = nc.scalar
            a.wait_ge(zi_, n)
            k = place(d, s)
            a.activation(gates[d][:, s % 2, 0:3 * B], z_ifg[d][s // SEED][:, k * 3 * B:(k + 1) * 3 * B], ACT.Tanh, scale=1 / S).then_inc(ai_, 1)
            a.wait_ge(zo_, n)
            a.activation(tho[d][:], z_o[d][:, k * B:(k + 1) * B], ACT.Tanh, scale=1 / S).then_inc(ao_, 1)

        def act_cell(d, slot, at_, dc_, n):
            nc.scalar.wait_ge(dc_, n)
            nc.scalar.activation(tc[d][:], gates[d][:, 1 - slot, 3 * B:4 * B], ACT.Tanh, scale=0.5).then_inc(at_, 1)

        @block.scalar
        def _(act):
            act.wait_ge(dh[1], 1)
            nc.scalar.activation(tc[0][:], h32[1][:], ACT.Tanh).then_inc(ao[1], 1)
            def embed(h, r, q, t, x):
                c = r + SEED * q
                if t:
                    if h == 3:
                        act.wait_ge(e_t4, c + SEED * 7)
                        if not isinstance(c, int) or c > -SEED * LEAD:
                            act.wait_ge(e_split, c + SEED * 6)
                        if not isinstance(c, int) or c > -SEED * (LEAD - 1):
                            act.wait_ge(e_conv, c + SEED * 5)
                        nc.scalar.activation(rowsT[0:D, 4 * P:5 * P], pB[0:D, 0:P], ACT.Copy, scale=SX)
                        nc.scalar.activation(rT_hi[0:D, q, 4 * P:5 * P], pB[0:D, 0:P], ACT.Copy, scale=SX).then_inc(e_r4, SEED)
                    if h == 5:
                        act.wait_ge(e_tr, c + SEED * 7)
                        nc.scalar.activation(rowsT[:, 0:2 * P], pA[:, 0:2 * P], ACT.Copy, scale=SX)
                        nc.scalar.activation(rT_hi[:, q, 0:P], pA[:, 0:P], ACT.Copy, scale=SX)
                    if h == 6:
                        nc.scalar.activation(rT_hi[:, q, P:3 * P], pA[:, P:3 * P], ACT.Copy, scale=SX)
                        nc.scalar.activation(rowsT[:, 2 * P:3 * P], pA[:, 2 * P:3 * P], ACT.Copy, scale=SX)
                    if h == 7:
                        nc.scalar.activation(rowsT[:, 3 * P:4 * P], pA[:, 3 * P:4 * P], ACT.Copy, scale=SX)
                        nc.scalar.activation(rT_hi[:, q, 3 * P:4 * P], pA[:, 3 * P:4 * P], ACT.Copy, scale=SX).then_inc(e_evac, SEED)
                if x and h == 4:
                    col = r * (P // STEPS) + 3 * P if q else (NCH - 1) * P - r * (P // STEPS)
                    act.wait_ge(e_xnT, c + SEED * 4)
                    nc.scalar.activation(xT[:, bass.ds(col, P)], pB[:, P:P + P // 2].bitcast(F16), ACT.Copy).then_inc(e_xT, SEED)

            def pair(i, t, x):
                for s in range(STEPS):
                    for d in range(2):
                        act_step(d, s, zi[d], zo[d], ai[d], ao[d], at[d], dc[d], i + s + 1)
                        embed(2 * (s % SEED) + d, i, s // SEED, t, x[s // SEED])
                        act_cell(d, s % 2, at[d], dc[d], i + s + 1)

            act.wait_ge(s_const, 4)
            for j in range(-LEAD, 0):
                for h in range(8):
                    embed(h, j // 2 * STEPS, j % 2, True, j >= -3)
                if j == -5:
                    act.wait_ge(s_lstm, 16 * 10)
                    for k in (UF, UB, WF, WB):
                        nc.scalar.activation(raw[:, k, G], raw[:, k, G], ACT.Copy, scale=2.0).then_inc(s_scaled, 1)
                    act.wait_ge(s_scaled, 4)
                    for k in (UF, UB, WF, WB):
                        nc.scalar.activation(raw[:, k, :], raw[:, k, :], ACT.Copy, scale=FACT[k]).then_inc(s_scaled, 1)
                    act.wait_ge(s_scaled, 8)
                    for k in (UF, UB, WF, WB):
                        nc.scalar.activation(hi[:, k, :], raw[:, k, :], ACT.Copy).then_inc(s_scaled, 1)
            with act.Fori(0, T // 2 - 4 * STEPS, BODY * STEPS) as i:
                for k in range(BODY):
                    pair(i + k * STEPS, True, (True, True))
            pair(T // 2 - 4 * STEPS, True, (True, True))
            pair(T // 2 - 3 * STEPS, False, (True, True))
            pair(T // 2 - 2 * STEPS, False, (True, False))
            pair(T // 2 - STEPS, False, (False, False))
            with act.Fori(T // 2, T, BODY * STEPS) as i:
                for k in range(BODY):
                    pair(i + k * STEPS, False, (False, False))

            def relu1(i, j):
                if j == PAIRS:
                    act.wait_ge(f_l1, i + 1)
                nc.scalar.activation(g1[:, j, :], pB[:, j * P:(j + 1) * P], ACT.Relu).then_inc(f_g1[j], 1)

            def relu2(i, j):
                if j == 0:
                    act.wait_ge(f_l2, i + 1)
                nc.scalar.activation(g2[:, j, :], pC[:, j * P:(j + 1) * P], ACT.Relu, bias=b2[:, j:j + 1]).then_inc(f_g2[j], 1)

            def chunk(i, steps, first, second):
                for s in range(STEPS):
                    if steps:
                        act_step(0, s, dzi, dzo, dai, dao, dat, ddc, i * STEPS + s + 1)
                    if first and s == 7:
                        relu2(i - 1, 0)
                        relu2(i - 1, 1)
                    if steps:
                        act_cell(0, s % 2, dat, ddc, i * STEPS + s + 1)
                    if second and s == 1:
                        act.wait_ge(f_route[7], i - 1)
                        nc.scalar.activation(pe_[:], pd[:], ACT.Exp).then_inc(f_pe, 1)
                    if first:
                        if s == 2:
                            act.wait_ge(f_tr, i)
                            nc.scalar.activation(fxT[:], pA[:, P:2 * P], ACT.Copy).then_inc(f_fxT, 1)
                        if s == 4:
                            relu1(i - 1, PAIRS)
                            relu1(i - 1, 0)
                        if s == 5:
                            relu1(i - 1, 1)
                            relu1(i - 1, 2)
                        if s == 6:
                            act.wait_ge(f_route[1], i)
                            nc.scalar.activation(ex[:], dl[:], ACT.Exp, accum_out=exs[:]).then_inc(f_ex, 1)
                        if s == 7:
                            relu2(i - 1, 2)

            chunk(0, True, False, False)
            chunk(1, True, True, False)
            chunk(2, True, True, True)
            with act.Fori(3, NCH) as i:
                chunk(i, True, True, True)
            chunk(NCH, False, True, True)
            chunk(NCH + 1, False, False, True)

        def mm(o, l, r, start=False):
            return nc.tensor.matmul(o, l, r, start=start, stop=True, skip_group_check=True)

        def z_of(d, g, half, k, n=1):
            if g < 3:
                v = z_ifg[d][half][:, 0:SEED * 3 * B].rearrange("p (k c) -> p k c", c=3 * B)
                return v[:, k:k + n, g * B:(g + 1) * B]
            return z_o[d][:, k * B:(k + n) * B].rearrange("p (k c) -> p k c", c=B)

        def recur(d, uj, s, zi_, zo_, dhi_, dlo_, n):
            gate = [slice(g * H, (g + 1) * H) for g in range(4)]
            z = [z_of(d, g, s // SEED, place(d, s)) for g in range(4)]
            prev = (s - 1) % STEPS
            nc.tensor.wait_ge(dhi_, n)
            for g in range(4):
                mm(z[g], hi[:, uj, gate[g]], hhi[d][:, prev, :])
                mm(z[g], lo[:, uj, gate[g]], hhi[d][:, prev, :])
            nc.tensor.wait_ge(dlo_, n)
            for g in range(4):
                last = mm(z[g], hi[:, uj, gate[g]], hlo[d][:, prev, :])
                if g == 2:
                    last.then_inc(zi_, 1)
                if g == 3:
                    last.then_inc(zo_, 1)

        def seed_input(d, g, half, col):
            x = xT[:, bass.ds(col, SEED * B)]
            cols = slice(g * H, (g + 1) * H)
            z = z_of(d, g, half, 0, SEED)
            mm(z, bpart[:, ENC_B[d], cols], ones[:, 0:SEED * B], start=g in (0, 3))
            mm(z, hi[:, WF + d, cols], x)
            mm(z, lo[:, WF + d, cols], x)

        def seed_const(part, half):
            if part < 2:
                ifg = z_ifg[0][half][:, 0:SEED * 3 * B].rearrange("p (k c) -> p k c", c=3 * B)
                mm(ifg, ident16[:], (zc_hi, zc_lo)[part][:, :, 0:3 * B], start=part == 0)
            else:
                o = z_o[0][:, 0:SEED * B].rearrange("p (k c) -> p k c", c=B)
                mm(o, ident16[:], zc_hi[:, :, 3 * B:4 * B], start=True)
                mm(o, ident16[:], zc_lo[:, :, 3 * B:4 * B])

        @block.tensor
        def _(pe):
            PRODUCTS = [(m, k) for m in range(NK) for k in range(3)]

            def embed(h, i, q, t, c, x):
                if not (t or c or x):
                    return
                j = i * 2 + q
                later = not isinstance(j, int)
                if h == 2 and (later or j > -5):
                    pe.wait_ge(e_hx, SEED * (j + 5 if later else min(j + 5, NCH)))
                if x and h == 2:
                    pe.wait_ge(e_xn, SEED * (j + 4))
                    nc.tensor.transpose(pB[:, P:P + P // 2].bitcast(F16), xn[:], ident16[:]).then_inc(e_xnT, SEED)
                if t and h < 5:
                    if h == 0:
                        pe.wait_ge(s_rows[q], i * 16 + 64)
                        if later or j > -LEAD:
                            pe.wait_ge(e_evac, SEED * (j + 6))
                    if h == 2:
                        nc.tensor.transpose(pB[0:D, 0:P], rows[:, q, (NK - 1) * P:GK], ident[:]).then_inc(e_t4, SEED)
                    else:
                        m = h if h < 2 else h - 1
                        tr = nc.tensor.transpose(pA[:, m * P:(m + 1) * P], rows[:, q, m * P:(m + 1) * P], ident[:])
                        if h == 4:
                            tr.then_inc(e_tr, SEED)
                if c and h >= 5:
                    if h == 5:
                        pe.wait_ge(e_split, SEED * (j + 6))
                        if t:
                            pe.wait_ge(e_r4, SEED * (j + 7))
                        if x:
                            pe.wait_ge(e_xT, SEED * (j + 4))
                    for m, k in PRODUCTS[(h - 5) * 5:(h - 4) * 5]:
                        rows_k = D if m == NK - 1 else P
                        last = mm(pB[:, 2 * P:2 * P + D], (rT_hi[:, 1 - q, :], rT_hi[:, 1 - q, :], rT_lo[:])[k][0:rows_k, m * P:(m + 1) * P],
                                  (cw_hi, cw_lo, cw_hi)[k][0:rows_k, m, :], start=(m, k) == (0, 0))
                    if h == 7:
                        last.then_inc(e_conv, SEED)

            def pair(i, t, c, x):
                for s in range(STEPS):
                    n = i * STEPS + s + 1
                    half = s // SEED
                    hs = 2 * (s % SEED)
                    if s == SEED and x[0]:
                        pe.wait_ge(e_xT, SEED * (i * 2 + 4))
                    recur(0, UF, s, zi[0], zo[0], dhi[0], dlo[0], n)
                    if s % SEED == 0:
                        pe.wait_ge(ao[1], n)
                        seed_input(1, 3, half, (NCH - i) * P + (1 - half) * SEED * B)
                    else:
                        seed_input(1, s % SEED - 1, 1 - half, (NCH - i) * P - half * SEED * B)
                    embed(hs, i, half, t, c[half], x[half])
                    recur(1, UB, s, zi[1], zo[1], dhi[1], dlo[1], n)
                    if s % SEED == SEED - 1:
                        pe.wait_ge(ao[0], n)
                    seed_input(0, s % SEED, 1 - half, i * P + (P + (half + 1) * SEED * B))
                    embed(hs + 1, i, half, t, c[half], x[half])

            pe.wait_ge(s_const, 2)
            for j in range(-LEAD, 0):
                if j == -5:
                    pe.wait_ge(s_cw, 6)
                if j == -3:
                    pe.wait_ge(s_const, 6)
                for h in range(8):
                    embed(h, j // 2, j % 2, True, j >= -5, j >= -3)
            pe.wait_ge(s_prep, PREP)
            pe.wait_ge(s_const, 9)
            for d in range(2):
                for g in range(4 if d == 0 else 3):
                    seed_input(d, g, 0, P if d == 0 else NCH * P + SEED * B)
            with pe.Fori(0, (NCH // 2 - 4) // BODY) as i:
                for k in range(BODY):
                    pair(BODY * i + k, True, (True, True), (True, True))
            pair(NCH // 2 - 4, True, (True, True), (True, True))
            pair(NCH // 2 - 3, False, (True, False), (True, True))
            pair(NCH // 2 - 2, False, (False, False), (True, False))
            pair(NCH // 2 - 1, False, (False, False), (False, False))
            with pe.Fori(NCH // 2 // BODY, NCH // BODY) as i:
                for k in range(BODY):
                    pair(BODY * i + k, False, (False, False), (False, False))
            pe.wait_ge(s_prep2, PREP2)
            for d in range(2):
                pe.wait_ge(dhi[d], T + 1)
                pe.wait_ge(dlo[d], T + 1)
            for g in range(4):
                cols = slice(g * H, (g + 1) * H)
                o = pA[:, g * B:(g + 1) * B]
                mm(o, bpart[:, DEC_B, cols], ones[:, 0:B], start=g == 0)
                for d in range(2):
                    mm(o, hi[:, WDF + d, cols], hhi[d][:, STEPS - 1, :])
                    mm(o, lo[:, WDF + d, cols], hhi[d][:, STEPS - 1, :])
                    last = mm(o, hi[:, WDF + d, cols], hlo[d][:, STEPS - 1, :])
            last.then_inc(s_zc, 1)
            pe.wait_ge(s_zcs, 3)
            for part in range(3):
                seed_const(part, 0)

            def l1(i, j):
                if j == PAIRS:
                    pe.wait_ge(f_fxT, i + 1)
                m = mm(pB[:, j * P:(j + 1) * P], w1[:, j, :], fxT[:], start=True)
                if j == PAIRS - 1:
                    m.then_inc(f_l1, 1)

            def chunk(i, steps, first, second):
                for s in range(STEPS):
                    if steps:
                        n = i * STEPS + s + 1
                        recur(0, UD, s, dzi, dzo, ddhi, ddlo, n)
                        if s % SEED < 2:
                            seed_const(s % SEED, 1 - s // SEED)
                    if first:
                        if s == 0:
                            if not steps:
                                pe.wait_ge(ddlo, i * STEPS + 1)
                            h_hi = hhi[0][:].rearrange("p s b -> p (s b)")
                            h_lo = hlo[0][:].rearrange("p s b -> p (s b)")
                            mm(pA[:, 0:D], h_hi, hi[:, WO, 0:D], start=True)
                            mm(pA[:, 0:D], h_hi, lo[:, WO, 0:D])
                            mm(pA[:, 0:D], h_lo, hi[:, WO, 0:D]).then_inc(f_proj, 1)
                        if s == 2:
                            pe.wait_ge(f_fx, i)
                            nc.tensor.transpose(pA[:, P:2 * P], fx[:], ident[:]).then_inc(f_tr, 1)
                        if s == 3:
                            l1(i - 1, PAIRS)
                            l1(i - 1, 0)
                        if s == 4:
                            l1(i - 1, 1)
                            l1(i - 1, 2)
                        if s == 5:
                            pe.wait_ge(f_g1[PAIRS], i)
                            mm(pA[:, 3 * P:3 * P + NPAD], g1[:, PAIRS, :], wr2[:], start=True).then_inc(f_lg, 1)
                            pe.wait_ge(f_g1[0], i)
                            mm(pC[:, 0:P], w2[:, 0, :], g1[:, 0, :], start=True)
                        if s == 6:
                            pe.wait_ge(f_g1[2], i)
                            mm(pC[:, P:2 * P], w2[:, 1, :], g1[:, 1, :], start=True)
                            mm(pC[:, 2 * P:3 * P], w2[:, 2, :], g1[:, 2, :], start=True).then_inc(f_l2, 1)
                    if second:
                        if s == 0:
                            if not (isinstance(i, int) and i == 2):
                                pe.wait_ge(f_comb[NE - 1], i - 2)
                            mm(pD[:, 0:NE * D], ones[:], bpart[:, E3_B, 0:NE * D], start=True)
                            pe.wait_ge(f_g2[PAIRS - 1], i - 1)
                            mm(pD[:, 0:P], g2[:, 0, :], w3[:, 0, :])
                        if s == 1:
                            mm(pD[:, P:2 * P], g2[:, 1, :], w3[:, 1, :])
                            mm(pD[:, 2 * P:3 * P], g2[:, 2, :], w3[:, 2, :]).then_inc(f_l3, 1)
                    if steps and s % SEED == SEED - 1:
                        pe.wait_ge(dao, n)
                        seed_const(2, None)

            pe.wait_ge(s_ffw, FFW)
            pe.wait_ge(s_const, 18)
            chunk(0, True, False, False)
            chunk(1, True, True, False)
            chunk(2, True, True, True)
            with pe.Fori(3, NCH) as i:
                chunk(i, True, True, True)
            chunk(NCH, False, True, True)
            chunk(NCH + 1, False, False, True)

        @block.vector
        def _(dve):
            v = nc.vector
            done = [0]

            def prep(ins, chain=True):
                done[0] += 1
                ins.then_inc(s_prep, 1)
                if chain:
                    dve.wait_ge(s_prep, done[0])

            def wait_apart(count, n):
                dve.wait_ge(s_ids, 16)
                dve.wait_ge(count, n)

            dve.wait_ge(s_ids, 16)
            v.tensor_scalar(idx_f[:], idx_in[:], float(-HALF), float(VOCAB - 1 + HALF), ALU.max, ALU.min).then_inc(s_idx, 1)
            dve.wait_ge(s_idx, 1)
            v.tensor_scalar(idx_f[:], idx_f[:], float(PAD - HALF), None, ALU.add).then_inc(s_idx, 1)
            dve.wait_ge(s_idx, 2)
            v.tensor_copy(idx[:], idx_f[:]).then_inc(s_idx, 1)
            v.memset(brow[:], 0.0).then_inc(s_zero, 1)
            v.memset(bpart[:], 0.0).then_inc(s_zero, 1)
            for d in range(2):
                if d == 1:
                    v.memset(h32[d][:], 0.0).then_inc(dh[d], 1)
                prep(v.memset(gates[d][:], 0.0), False)
                if d == 0:
                    v.memset(hlo[d][:], 0.0).then_inc(dlo[d], 1)
                v.memset(hhi[d][:], 0.0).then_inc(dhi[d], 1)
            dve.wait_ge(s_conv, 64)
            for m, k in ((slice(0, NK - 1), P), (slice(NK - 1, NK), D)):
                v.tensor_scalar(convw[0:k, m, :], convw[0:k, m, :], SW, None, ALU.mult).then_inc(s_cw, 1)
            dve.wait_ge(s_cw, 2)
            for m, k in ((slice(0, NK - 1), P), (slice(NK - 1, NK), D)):
                v.tensor_copy(cw_hi[0:k, m, :], convw[0:k, m, :]).then_inc(s_cw, 1)
            dve.wait_ge(s_cw, 4)
            for m, k in ((slice(0, NK - 1), P), (slice(NK - 1, NK), D)):
                v.tensor_tensor(cw_lo[0:k, m, :], convw[0:k, m, :], cw_hi[0:k, m, :], ALU.subtract).then_inc(s_cw, 1)

            def embed(h, r, q, steps):
                c = r + SEED * (q + 5)
                if h == 0:
                    dve.wait_ge(e_conv, c)
                    v.scalar_tensor_tensor(out=hx[:], in0=pB[:, 2 * P:2 * P + D], scalar=1 / (SX * SW), in1=convb[:],
                                           op0=ALU.mult, op1=ALU.add).then_inc(e_hx, SEED)
                if h == 1:
                    if not steps:
                        dve.wait_ge(e_hx, c)
                    v.bn_stats(st[:], hx[:]).then_inc(e_st, SEED)
                if h == 2:
                    if not steps:
                        dve.wait_ge(e_st, c)
                    v.bn_aggr(mv[:], st[:]).then_inc(e_mv, SEED)
                if h == 3:
                    if not steps:
                        dve.wait_ge(e_mv, c)
                    v.tensor_scalar(ve[:], mv[:, 1:2], EPS, None, ALU.add).then_inc(e_ve, SEED)
                if h == 5:
                    dve.wait_ge(e_rstd, c)
                    v.tensor_scalar(xn32[:], hx[:], mv[:, 0:1], rstd[:], ALU.subtract, ALU.mult).then_inc(e_xn32, SEED)
                if h == 6:
                    if not isinstance(c, int) or c > SEED:
                        dve.wait_ge(e_xnT, c - SEED)
                    if not steps:
                        dve.wait_ge(e_xn32, c)
                    v.tensor_copy(xn[:, 0:D], xn32[:]).then_inc(e_xn, SEED // 2)
                if h == 7:
                    if not steps:
                        dve.wait_ge(e_xn, c - SEED // 2)
                    v.tensor_tensor(xn[:, D:2 * D], xn32[:], xn[:, 0:D], ALU.subtract).then_inc(e_xn, SEED // 2)

            EB = slice(0, 2)
            for j in range(-4, 0):
                for h in range(8):
                    embed(h, j // 2 * STEPS, j % 2, False)
                    if h == 3 and j == -3:
                        dve.wait_ge(s_small, 16 * 12)
                        dve.wait_ge(s_zero, 2)
                        prep(v.tensor_scalar(brow[:, EB, :], brow[:, EB, :], S / 2, None, ALU.mult), False)
                    if h == 3 and j == -2:
                        dve.wait_ge(s_prep, done[0])
                        prep(v.tensor_scalar(brow[:, EB, G], brow[:, EB, G], 2.0, None, ALU.mult))
                        prep(v.tensor_copy(bp_hi[:, EB, :], brow[:, EB, :]), False)
                    if h == 3 and j == -1:
                        dve.wait_ge(s_prep, done[0])
                        prep(v.tensor_tensor(brest[:, EB, :], brow[:, EB, :], bp_hi[:, EB, :], ALU.subtract), False)
                if j == -4:
                    dve.wait_ge(s_scaled, 3 * 4)
                k = (UF, UB, WF, WB)[j + 4]
                prep(v.tensor_tensor(lo[:, k, :], raw[:, k, :], hi[:, k, :], ALU.subtract), False)
            dve.wait_ge(s_prep, done[0])
            prep(v.tensor_copy(bp_mid[:, EB, :], brest[:, EB, :]), False)
            prep(v.tensor_copy(bpart[0:1, EB, :], bp_hi[0:1, EB, :]), False)
            dve.wait_ge(s_prep, done[0] - 1)
            prep(v.tensor_copy(bpart[32:33, EB, :], bp_mid[32:33, EB, :]), False)
            prep(v.tensor_tensor(bpart[64:65, EB, :], brest[64:65, EB, :], bp_mid[64:65, EB, :], ALU.subtract), False)
            assert done[0] == PREP, done[0]

            def products(d, slot, ai_, dp_, n):
                dve.wait_ge(ai_, n)
                v.scalar_tensor_tensor(out=prod[d][:], in0=gates[d][:, slot, 0:2 * B], scalar=1.0,
                                       in1=gates[d][:, slot, 2 * B:4 * B], op0=ALU.add, op1=ALU.mult).then_inc(dp_, 1)

            def cell(d, slot, dp_, dc_, n):
                dve.wait_ge(dp_, n)
                v.scalar_tensor_tensor(out=gates[d][:, 1 - slot, 3 * B:4 * B], in0=prod[d][:, B:2 * B], scalar=0.5,
                                       in1=prod[d][:, 0:B], op0=ALU.mult, op1=ALU.add).then_inc(dc_, 1)

            def hidden(d, s, at_, dhi_, dh_, n):
                dve.wait_ge(at_, n)
                v.scalar_tensor_tensor(out=hhi[d][:, s, :], in0=tho[d][:], scalar=1.0, in1=tc[d][:],
                                       op0=ALU.add, op1=ALU.mult).then_inc(dhi_, 1)
                v.scalar_tensor_tensor(out=h32[d][:], in0=tho[d][:], scalar=1.0, in1=tc[d][:],
                                       op0=ALU.add, op1=ALU.mult).then_inc(dh_, 1)

            def low(d, s, dh_, dlo_, n):
                dve.wait_ge(dh_, n)
                v.tensor_tensor(hlo[d][:, s, :], h32[d][:], hhi[d][:, s, :], ALU.subtract).then_inc(dlo_, 1)

            def pair(i, norm):
                for s in range(STEPS):
                    n = i + s + 1
                    for d in range(2):
                        products(d, s % 2, ai[d], dp[d], n)
                        if d == 0:
                            low(1, (s - 1) % STEPS, dh[1], dlo[1], n)
                        else:
                            low(0, s, dh[0], dlo[0], n)
                        cell(d, s % 2, dp[d], dc[d], n)
                        if norm:
                            embed(2 * (s % SEED) + d, i, s // SEED, True)
                        hidden(d, s, at[d], dhi[d], dh[d], n)

            with dve.Fori(0, T // 2 - 4 * STEPS, BODY * STEPS) as i:
                for k in range(BODY):
                    pair(i + k * STEPS, True)
            for k in (4, 3, 2, 1):
                pair(T // 2 - k * STEPS, k > 2)
            with dve.Fori(T // 2, T, BODY * STEPS) as i:
                for k in range(BODY):
                    pair(i + k * STEPS, False)
            dve.wait_ge(e_h1, SEED * NCH)
            dve.wait_ge(s_const, 18)
            low(1, STEPS - 1, dh[1], dlo[1], T + 1)

            dve.wait_ge(s_zc, 1)
            v.tensor_copy(zc32[:], pA[:, 0:4 * B]).then_inc(s_zcs, 1)
            dve.wait_ge(s_zcs, 1)
            zc_b = zc32[:].rearrange("p (a c) -> p a c", a=1).broadcast_to([P, SEED, 4 * B])
            v.tensor_copy(zc_hi[:], zc_b).then_inc(s_zcs, 1)
            dve.wait_ge(s_zcs, 2)
            v.memset(gates[0][:], 0.0).then_inc(s_prep, 1)
            v.memset(hlo[0][:], 0.0).then_inc(ddlo, 1)
            v.memset(hhi[0][:], 0.0).then_inc(ddhi, 1)
            v.tensor_tensor(zc_lo[:], zc_b, zc_hi[:], ALU.subtract).then_inc(s_zcs, 1)
            dve.wait_ge(s_prep, PREP + 1)

            def route(n, k, apart=False):
                (wait_apart if apart else dve.wait_ge)(f_route[k - 2], n)

            def chunk(i, steps, first, second):
                for s in range(STEPS):
                    n = i * STEPS + s + 1
                    if steps:
                        products(0, s % 2, dai, ddp, n)
                        cell(0, s % 2, ddp, ddc, n)
                    a, b = i - 1, i - 2
                    if first:
                        if s == 1:
                            wait_apart(f_st, i)
                            v.bn_aggr(mv[:], st[:]).then_inc(f_mv, 1)
                        if s == 2:
                            dve.wait_ge(f_rstd, i)
                            v.tensor_scalar(fx[:, 0:D], y1[:], mv[:, 0:1], rstd[:], ALU.subtract, ALU.mult).then_inc(f_fx, 1)
                        if s == 7:
                            v.tensor_copy(yres[:], y1[:]).then_inc(f_yres, 1)
                        if s == 6:
                            route(i, 2)
                            v.tensor_scalar(dl[:], pA[:, 3 * P:3 * P + NPAD], m8[:, 0:1], None, ALU.subtract).then_inc(f_route[1], 1)
                        if s == 7:
                            dve.wait_ge(f_ex, i)
                            v.reciprocal(exr[:], exs[:]).then_inc(f_route[2], 1)
                    if second:
                        if s == 0:
                            if first:
                                dve.wait_ge(f_proj, i)
                            route(i - 1, 4)
                            v.tensor_scalar(pr[:], ex[:], exr[:], None, ALU.mult).then_inc(f_route[3], 1)
                        if s == 1:
                            route(i - 1, 6)
                            v.tensor_tensor(pd[:], p8[:, 1:2], p8[:, 0:1], ALU.subtract).then_inc(f_route[7], 1)
                        if s == 2:
                            route(i - 1, 7)
                            v.tensor_copy(topf[:], top[:]).then_inc(f_route[6], 1)
                        if s == 3:
                            route(i - 1, 11)
                            v.tensor_scalar(rw0[:], iota[:], topf[:, 0:1], wt0[:], ALU.is_equal, ALU.mult).then_inc(f_route[10], 1)
                            v.tensor_tensor(wt1[:], pe_[:], wt0[:], ALU.mult).then_inc(f_route[11], 1)
                        if 4 <= s < 7:
                            comb(b, 2 * (s - 4))
                    if steps:
                        if s == 0 and first and not second:
                            dve.wait_ge(f_proj, i)
                        hidden(0, s, dat, ddhi, ddh, n)
                        low(0, s, ddh, ddlo, n)
                    if second and s == 0:
                        route(i - 1, 5, apart=True)
                        v.max(p8[:], pr[:]).then_inc(f_route[4], 1)
                    if second:
                        if s == 1:
                            v.max_index(top[:], p8[:], pr[:]).then_inc(f_route[5], 1)
                        if s == 2:
                            dve.wait_ge(f_pe, i - 1)
                            v.tensor_scalar(pden[:], pe_[:], 1.0, None, ALU.add).then_inc(f_route[8], 1)
                            route(i - 1, 10)
                            v.reciprocal(wt0[:], pden[:]).then_inc(f_route[9], 1)
                        if s == 3:
                            route(i - 1, 13)
                            v.tensor_scalar(rw1[:], iota[:], topf[:, 1:2], wt1[:], ALU.is_equal, ALU.mult).then_inc(f_route[12], 1)
                            route(i - 1, 14)
                            v.tensor_tensor(rw[:], rw0[:], rw1[:], ALU.add).then_inc(f_route[13], 1)
                        if 4 <= s < 7:
                            comb(b, 2 * (s - 4) + 1)
                    if first:
                        if s == 0:
                            dve.wait_ge(f_proj, i)
                            if second:
                                dve.wait_ge(f_yres, i - 1)
                            v.scalar_tensor_tensor(out=y1[:], in0=pA[:, 0:D], scalar=1 / S,
                                                   in1=h1[:, bass.ds(a, 1), :].rearrange("p c d -> p (c d)"),
                                                   op0=ALU.mult, op1=ALU.add).then_inc(f_y1, 1)
                            dve.wait_ge(f_y1, i)
                            v.bn_stats(st[:], y1[:]).then_inc(f_st, 1)
                        if s == 1:
                            dve.wait_ge(f_mv, i)
                            v.tensor_scalar(ve[:], mv[:, 1:2], EPS, None, ALU.add).then_inc(f_ve, 1)
                        if s == 5:
                            wait_apart(f_lg, i)
                            v.max(m8[:], pA[:, 3 * P:3 * P + NPAD]).then_inc(f_route[0], 1)

            def comb(b, e):
                if e == 0:
                    dve.wait_ge(f_l3, b + 1)
                    dve.wait_ge(f_route[ROUTE - 1], b + 1)
                    dve.wait_ge(f_yres, b + 1)
                else:
                    dve.wait_ge(f_comb[e - 1], b + 1)
                if e == NE - 1 and not (isinstance(b, int) and b == 0):
                    dve.wait_ge(s_out, 16 * b)
                v.scalar_tensor_tensor(out=yout[:] if e == NE - 1 else acc[:], in0=pD[:, e * D:(e + 1) * D],
                                       scalar=rw[:, e:e + 1], in1=yres[:] if e == 0 else acc[:],
                                       op0=ALU.mult, op1=ALU.add).then_inc(f_comb[e], 1)

            chunk(0, True, False, False)
            chunk(1, True, True, False)
            chunk(2, True, True, True)
            with dve.Fori(3, NCH) as i:
                chunk(i, True, True, True)
            chunk(NCH, False, True, True)
            chunk(NCH + 1, False, False, True)


ROUTE = 14
PREP = 2 + 4 + 8
PREP2 = 3 * 4 + 3 + 8

_IN = ["L0_tok_b", "L0_attn_Wf", "L0_attn_Uf", "L0_attn_bf", "L0_attn_Wb", "L0_attn_Ub", "L0_attn_bb",
       "L0_attn_Wd", "L0_attn_Ud", "L0_attn_bd", "L0_attn_Wo", "L0_attn_bo", "L0_ffn_router_w1",
       "L0_ffn_router_b1", "L0_ffn_router_w2", "L0_ffn_router_b2", "L0_ffn_expert_w1", "L0_ffn_expert_b1",
       "L0_ffn_expert_w2", "L0_ffn_expert_b2", "L0_ffn_expert_w3", "L0_ffn_expert_b3"]


def kernel(**inputs):
    import numpy as np
    import concourse.bacc as bacc
    from concourse.bass_utils import run_bass_kernel_spmd as run

    nc = bacc.Bacc("TRN2", target_bir_lowering=False, num_devices=1)
    a = {k: np.ascontiguousarray(inputs[k]) for k in _IN}
    a["ids"] = np.ascontiguousarray(np.asarray(inputs["x"]).reshape(B, NCH, STEPS).transpose(2, 0, 1).reshape(P, NCH))
    emb = np.asarray(inputs["L0_tok_emb"])
    a["table"] = np.concatenate([np.repeat(emb[:1], PAD, axis=0), emb, np.repeat(emb[-1:], PAD, axis=0)])
    a["L0_ffn_expert_b2"] = np.ascontiguousarray(a["L0_ffn_expert_b2"].reshape(PAIRS, P).T)
    a["conv_w"] = np.ascontiguousarray(np.asarray(inputs["L0_tok_W"]).transpose(2, 1, 0))
    t = {k: nc.dram_tensor("in_" + k, x.shape, mybir.dt.from_np(x.dtype), kind="ExternalInput").ap() for k, x in a.items()}
    o = nc.dram_tensor("out_h", (B, T, D), F32, kind="ExternalOutput").ap()
    at = lambda n: t["L0_attn_" + n]
    ff = lambda n: t["L0_ffn_" + n]
    tower(nc, t["ids"], t["table"], t["conv_w"], t["L0_tok_b"], (at("Wf"), at("Wb")), (at("Uf"), at("Ub")),
          (at("bf"), at("bb")), at("Wd"), at("Ud"), at("bd"), at("Wo"), at("bo"),
          ff("router_w1"), ff("router_b1"), ff("router_w2"), ff("router_b2"), ff("expert_w1"), ff("expert_b1"),
          ff("expert_w2"), ff("expert_b2"), ff("expert_w3"), ff("expert_b3"), o)
    r = run(nc, [{"in_" + k: x for k, x in a.items()}], core_ids=[0])
    return r.results[0]["out_h"]
```

```python
import math
from contextlib import ExitStack

import concourse.bass as bass
from concourse import mybir

F32 = mybir.dt.float32
F16 = mybir.dt.float16
BF16 = mybir.dt.bfloat16
I32 = mybir.dt.int32
U32 = mybir.dt.uint32
ALU = mybir.AluOpType
ACT = mybir.ActivationFunctionType

B, T = 16, 512
D = 64
KS = 9
H = 128
NE = 6
RH = 32
VOCAB = 50257
HALF = KS // 2
PAD = 2 * HALF
P = 128
STEPS = P // B
NCH = T // STEPS
SEED = STEPS // 2
GK = KS * D
NK = (GK + P - 1) // P
PAIRS = NE // 2
NPAD = 8
EPS = 1e-5
S = 512.0
HS = 4.0
ORDER = (0, 2, 3, 1)
SX = 256.0
SW = 256.0
BODY = 4
LEAD = 6
LEAST = -1.0e30


def tower(nc, ids, table, conv_w, conv_b, w_in, u_in, b_in, wd, ud, bd, wo, bo,
          r_w1, r_b1, r_w2, r_b2, e_w1, e_b1, e_w2, e_b2, e_w3, e_b3, out):
    with ExitStack() as ctx:
        def sb(name, shape, dt=F32):
            return ctx.enter_context(nc.sbuf_tensor(name, shape, dt))

        def bank(name, dt=F32):
            return ctx.enter_context(nc.psum_tensor(name, [P, 2048 // (4 if dt == F32 else 2)], dt))

        def sem(name):
            return ctx.enter_context(nc.semaphore(name))

        raw = sb("raw", [P, 8, 4 * H])
        hi = sb("hi", [P, 8, 4 * H], F16)
        lo = sb("lo", [P, 8, 4 * H], F16)
        brow = sb("brow", [P, 4, 4 * H])
        brest = sb("brest", [P, 4, 4 * H])
        bp_hi = sb("bp_hi", [P, 4, 4 * H], BF16)
        bp_mid = sb("bp_mid", [P, 4, 4 * H], BF16)
        bpart = sb("bpart", [P, 4, 4 * H], BF16)
        ones = sb("ones", [P, P], BF16)
        ident = sb("ident", [P, P])
        ident16 = sb("ident16", [P, P], F16)
        convw = sb("convw", [P, NK, D])
        cw_hi = sb("cw_hi", [P, NK, D], F16)
        cw_lo = sb("cw_lo", [P, NK, D], F16)
        convb = sb("convb", [P, D])
        bob = sb("bob", [P, D])
        w1 = sb("w1", [P, PAIRS + 1, P])
        w2 = sb("w2", [P, PAIRS, P])
        b2 = sb("b2", [P, PAIRS])
        w3 = sb("w3", [P, PAIRS, P])
        wr2 = sb("wr2", [P, NPAD])
        iota = sb("iota", [P, NPAD])
        halfneg = sb("halfneg", [P, 1])
        ebase = sb("ebase", [P, NPAD])
        idx_in = sb("idx_in", [P, NCH], I32)
        idx_f = sb("idx_f", [P, NCH])
        idx = sb("idx", [P, NCH], I32)
        rows = sb("rows", [P, 2, GK])
        idx_c = sb("idx_c", [P, 2], I32)
        rowsT = sb("rowsT", [P, NK * P])
        rT_hi = sb("rT_hi", [P, 2, NK * P], F16)
        rT_lo = sb("rT_lo", [P, NK * P], F16)
        h1 = sb("h1", [P, NCH, D])
        hx = sb("hx", [P, D])
        st = sb("st", [P, 6])
        mv = sb("mv", [P, 2])
        ve = sb("ve", [P, 1])
        rstd = sb("rstd", [P, 1])
        xn32 = sb("xn32", [P, D])
        xn = sb("xn", [P, 2 * D], F16)
        xT = sb("xT", [P, (NCH + 2) * P], F16)
        gf = [sb(f"gf{d}", [P, B]) for d in "fb"]
        gi = [sb(f"gi{d}", [P, B, 2]) for d in "fb"]
        gfc = [sb(f"gfc{d}", [P, B, 2]) for d in "fb"]
        cs = [sb(f"cs{d}", [P, B, 2]) for d in "fb"]
        go = [sb(f"go{d}", [P, B]) for d in "fb"]
        tc = [sb(f"tc{d}", [P, B]) for d in "fb"]
        h32 = [sb(f"h32{d}", [P, B]) for d in "fb"]
        hhi = [sb(f"hhi{d}", [P, STEPS, B], F16) for d in "fb"]
        hlo = [sb(f"hlo{d}", [P, STEPS, B], F16) for d in "fb"]
        zc32 = sb("zc32", [P, 4 * B])
        zc_hi = sb("zc_hi", [P, SEED, 4 * B], F16)
        zc_lo = sb("zc_lo", [P, SEED, 4 * B], F16)
        y1 = sb("y1", [P, D])
        yres = sb("yres", [P, D])
        acc = sb("acc", [P, D])
        yout = sb("yout", [P, D])
        fx = sb("fx", [P, P])
        fxT = sb("fxT", [P, P])
        g1 = sb("g1", [P, PAIRS + 1, P])
        g2 = sb("g2", [P, PAIRS, P])
        m8 = sb("m8", [P, NPAD])
        dl = sb("dl", [P, NPAD])
        ex = sb("ex", [P, NPAD])
        exs = sb("exs", [P, 1])
        exr = sb("exr", [P, 1])
        pr = sb("pr", [P, NPAD])
        p8 = sb("p8", [P, NPAD])
        top = sb("top", [P, NPAD], U32)
        topf = sb("topf", [P, NPAD])
        pd = sb("pd", [P, 1])
        wt0 = sb("wt0", [P, 1])
        wt1 = sb("wt1", [P, 1])
        rw0 = sb("rw0", [P, NPAD])
        rw1 = sb("rw1", [P, NPAD])
        rw = sb("rw", [P, NPAD])

        z_igo = [[bank(f"z_igo_{d}{k}") for k in range(2)] for d in "fb"]
        z_f = [bank("z_f_f"), bank("z_f_b")]
        pA, pB = bank("pA"), bank("pB")
        pC, pD = z_igo[1]

        s_ids = sem("s_ids")
        s_conv = sem("s_conv")
        s_small = sem("s_small")
        s_lstm = sem("s_lstm")
        s_ffw = sem("s_ffw")
        s_const = sem("s_const")
        s_idx = sem("s_idx")
        s_zero = sem("s_zero")
        s_scaled = sem("s_scaled")
        s_prep = sem("s_prep")
        s_rows = [sem("s_rows0"), sem("s_rows1")]
        s_cw = sem("s_cw")
        e_t4 = sem("e_t4")
        e_tr = sem("e_tr")
        e_r4 = sem("e_r4")
        e_evac = sem("e_evac")
        e_idx = sem("e_idx")
        e_split = sem("e_split")
        e_conv = sem("e_conv")
        e_hx = sem("e_hx")
        e_h1 = sem("e_h1")
        e_st = sem("e_st")
        e_mv = sem("e_mv")
        e_ve = sem("e_ve")
        e_rstd = sem("e_rstd")
        e_xn32 = sem("e_xn32")
        e_xn = sem("e_xn")
        e_xnT = sem("e_xnT")
        e_xT = sem("e_xT")
        s_prep2 = sem("s_prep2")
        zi = [sem("zi_f"), sem("zi_b")]
        af = [sem("af_f"), sem("af_b")]
        zf = [sem("zf_f"), sem("zf_b")]
        ai = [sem("ai_f"), sem("ai_b")]
        ao = [sem("ao_f"), sem("ao_b")]
        at = [sem("at_f"), sem("at_b")]
        dp = [sem("dp_f"), sem("dp_b")]
        dc = [sem("dc_f"), sem("dc_b")]
        dhi = [sem("dhi_f"), sem("dhi_b")]
        dh = [sem("dh_f"), sem("dh_b")]
        dlo = [sem("dlo_f"), sem("dlo_b")]
        s_zc = sem("s_zc")
        s_zcs = sem("s_zcs")
        daf = sem("daf")
        dzi, dzf, dai, dao, dat = sem("dzi"), sem("dzf"), sem("dai"), sem("dao"), sem("dat")
        ddp, ddc, ddhi, ddh, ddlo = sem("ddp"), sem("ddc"), sem("ddhi"), sem("ddh"), sem("ddlo")
        f_proj = sem("f_proj")
        f_y1 = sem("f_y1")
        f_st = sem("f_st")
        f_mv = sem("f_mv")
        f_ve = sem("f_ve")
        f_rstd = sem("f_rstd")
        f_fx = sem("f_fx")
        f_tr = sem("f_tr")
        f_fxT = sem("f_fxT")
        f_l1 = sem("f_l1")
        f_g1 = [sem(f"f_g1_{j}") for j in range(PAIRS + 1)]
        f_lg = sem("f_lg")
        f_l2 = sem("f_l2")
        f_g2 = [sem(f"f_g2_{j}") for j in range(PAIRS)]
        f_l3 = sem("f_l3")
        f_route = [sem(f"f_route{k}") for k in range(1, ROUTE + 1)]
        f_ex = sem("f_ex")
        f_exs = sem("f_exs")
        f_wt = sem("f_wt")
        f_yres = sem("f_yres")
        f_comb = [sem(f"f_comb{e}") for e in range(NE)]
        s_out = sem("s_out")

        block = ctx.enter_context(nc.Block())

        UF, UB, UD, WF, WB, WDF, WDB, WO = range(8)
        ENC_B, DEC_B, E3_B = (0, 1), 2, 3
        FFW = 16 * 11

        @block.sync
        def _(sp):
            sp.dma_start(idx_in[:], ids).then_inc(s_ids, 16)
            cw = conv_w.rearrange("k h o -> (k h) o")
            sp.dma_start(convw[:, 0:NK - 1, :], cw[0:(NK - 1) * P, :].rearrange("(m p) o -> p m o", p=P)).then_inc(s_conv, 16)
            sp.dma_start(convw[0:GK - (NK - 1) * P, NK - 1, :], cw[(NK - 1) * P:GK, :]).then_inc(s_conv, 16)
            sp.dma_start(convb[:], conv_b.rearrange("(a d) -> a d", a=1).broadcast_to([P, D])).then_inc(s_conv, 16)
            sp.dma_start(bob[:], bo.rearrange("(a d) -> a d", a=1).broadcast_to([P, D])).then_inc(s_conv, 16)
            for j, w in ((UF, u_in[0]), (UB, u_in[1]), (UD, ud)):
                sp.dma_start(raw[:, j, :], w).then_inc(s_lstm, 16)
            for j, w in ((WF, w_in[0]), (WB, w_in[1])):
                for q in range(2):
                    sp.dma_start(raw[q * D:(q + 1) * D, j, :], w).then_inc(s_lstm, 16)
            sp.dma_start(raw[:, WDF, :], wd[0:H, :]).then_inc(s_lstm, 16)
            sp.dma_start(raw[:, WDB, :], wd[H:2 * H, :]).then_inc(s_lstm, 16)
            sp.dma_start(raw[:, WO, 0:D], wo).then_inc(s_lstm, 16)
            sp.wait_ge(s_zero, 2)
            for q in (0, 32, 64):
                for j, b in enumerate((b_in[0], b_in[1], bd)):
                    sp.dma_start(brow[q:q + 1, j, :], b.rearrange("(a n) -> a n", a=1)).then_inc(s_small, 16)
                sp.dma_start(brow[q:q + 1, E3_B, 0:NE * D], e_b3.rearrange("(a e) d -> a (e d)", a=1)).then_inc(s_small, 16)
            sp.wait_ge(s_const, 14)
            sp.dma_start(w1[0:D, 0:PAIRS, :].rearrange("p j (q h) -> p (j q) h", q=2), e_w1.rearrange("e d h -> d e h")).then_inc(s_ffw, 16)
            sp.dma_start(w1[D:D + 1, 0:PAIRS, :].rearrange("p j c -> p (j c)"), e_b1.rearrange("(a e) h -> a (e h)", a=1)).then_inc(s_ffw, 16)
            sp.dma_start(w1[0:D, PAIRS, 0:RH], r_w1).then_inc(s_ffw, 16)
            sp.dma_start(w1[D:D + 1, PAIRS, 0:RH], r_b1.rearrange("(a n) -> a n", a=1)).then_inc(s_ffw, 16)
            for q in range(2):
                sp.dma_start(w2[q * D:(q + 1) * D, :, q * D:(q + 1) * D], e_w2.rearrange("(j q) h f -> q h j f", q=2)[q]).then_inc(s_ffw, 16)
                sp.dma_start(w3[q * D:(q + 1) * D, :, q * D:(q + 1) * D], e_w3.rearrange("(j q) h f -> q h j f", q=2)[q]).then_inc(s_ffw, 16)
            sp.dma_start(b2[:], e_b2).then_inc(s_ffw, 16)
            sp.dma_start(wr2[0:RH, 0:NE], r_w2).then_inc(s_ffw, 16)
            sp.dma_start(wr2[RH:RH + 1, 0:NE], r_b2.rearrange("(a n) -> a n", a=1)).then_inc(s_ffw, 16)
            out_c = out.rearrange("b (c t) d -> c t b d", t=STEPS)
            with sp.Fori(0, NCH) as c:
                sp.wait_ge(f_comb[NE - 1], c + 1)
                sp.dma_start(out_c[bass.ds(c, 1), :, :, :].rearrange("c t b d -> (c t) b d"), yout[:]).then_inc(s_out, 16)
            sp.wait_ge(s_out, 16 * NCH)

        @block.gpsimd
        def _(pool):
            pool.wait_ge(s_idx, 3)
            for c, col in enumerate((0, NCH - 1)):
                nc.gpsimd.indirect_dma_start(rows[:, c, :], None, table, bass.IndirectOffsetOnAxis(ap=idx[:, col:col + 1], axis=0)).then_inc(s_rows[c], 16)
            nc.gpsimd.memset(ident[:], 0.0).then_inc(s_const, 1)
            pool.wait_ge(s_const, 1)
            nc.gpsimd.affine_select(out=ident[:], in_=ident[:], compare_op=ALU.not_equal, fill=1.0, base=0,
                                    pattern=[[-1, P]], channel_multiplier=1).then_inc(s_const, 1)
            nc.gpsimd.memset(rowsT[:, (NK - 1) * P:NK * P], 0.0).then_inc(s_const, 1)
            nc.gpsimd.memset(rT_hi[:, :, (NK - 1) * P:NK * P], 0.0).then_inc(s_const, 1)
            nc.gpsimd.memset(halfneg[:], -0.5).then_inc(s_const, 1)
            pool.wait_ge(s_const, 2)
            nc.gpsimd.tensor_copy(ident16[:], ident[:]).then_inc(s_const, 1)
            nc.gpsimd.memset(xT[:, 0:P], 0.0).then_inc(s_const, 1)
            nc.gpsimd.memset(xT[:, (NCH + 1) * P:], 0.0).then_inc(s_const, 1)
            nc.gpsimd.memset(ones[:], 1.0).then_inc(s_const, 1)

            def wait_apart(count, n):
                pool.wait_ge(s_idx, 3)
                pool.wait_ge(count, n)

            def embed(j, i, q, t, c, n):
                if c:
                    pool.wait_ge(e_evac, SEED * (j + 6))
                    if not isinstance(j, int) or j > -5:
                        pool.wait_ge(e_conv, SEED * (j + 5))
                    nc.gpsimd.tensor_tensor(rT_lo[:], rowsT[:], rT_hi[:, 1 - q, :], ALU.subtract).then_inc(e_split, SEED)
                if n:
                    chunk = i + 2 if q == 0 else NCH - 3 - i
                    wait_apart(e_hx, SEED * (j + 5))
                    nc.gpsimd.tensor_tensor(h1[:, bass.ds(chunk, 1), :].rearrange("p c d -> p (c d)"), hx[:], bob[:], ALU.add).then_inc(e_h1, SEED)
                    if t:
                        pool.wait_ge(e_t4, SEED * (j + 7))
                    pool.wait_ge(e_ve, SEED * (j + 5))
                    nc.gpsimd.tensor_tensor(rstd[:], ve[:], halfneg[:], ALU.pow).then_inc(e_rstd, SEED)
                if t:
                    chunk = i + 4 if q == 0 else NCH - 5 - i
                    if not n:
                        pool.wait_ge(e_t4, SEED * (j + 7))
                    nc.gpsimd.tensor_copy(idx_c[:, q:q + 1], idx[:, bass.ds(chunk, 1)]).then_inc(e_idx, 1)
                    wait_apart(e_idx, j + LEAD + 1)
                    pool.wait_ge(e_tr, SEED * (j + 7))
                    nc.gpsimd.indirect_dma_start(rows[:, q, :], None, table, bass.IndirectOffsetOnAxis(ap=idx_c[:, q:q + 1], axis=0)).then_inc(s_rows[q], 16)

            def consts(k):
                if k == 0:
                    nc.gpsimd.memset(w1[:], 0.0).then_inc(s_const, 1)
                    nc.gpsimd.memset(wr2[:], 0.0).then_inc(s_const, 1)
                    nc.gpsimd.memset(fx[:], 0.0).then_inc(s_const, 1)
                if k == 1:
                    nc.gpsimd.memset(w2[:], 0.0).then_inc(s_const, 1)
                    nc.gpsimd.memset(w3[:], 0.0).then_inc(s_const, 1)
                if k == 2:
                    nc.gpsimd.memset(ebase[:], math.e).then_inc(s_const, 1)
                    nc.gpsimd.iota(iota[:], [[1, NPAD]], channel_multiplier=0, allow_small_or_imprecise_dtypes=True).then_inc(s_const, 1)
                    pool.wait_ge(s_const, 16)
                    nc.gpsimd.memset(fx[:, D:D + 1], 1.0).then_inc(s_const, 1)
                    pool.wait_ge(s_const, 17)
                    nc.gpsimd.memset(w1[D:D + 1, PAIRS, RH:RH + 1], 1.0).then_inc(s_const, 1)
                    pool.wait_ge(s_const, 18)
                    nc.gpsimd.memset(wr2[RH:RH + 1, NE:NPAD], LEAST).then_inc(s_const, 1)
                    pool.wait_ge(s_const, 19)

            for j in range(-LEAD, 0):
                embed(j, j // 2, j % 2, True, j >= -5, j >= -4)
                consts(j + LEAD)
            with pool.Fori(0, NCH // 2 - 4) as i:
                for q in range(2):
                    embed(2 * i + q, i, q, True, True, True)
            for j in range(NCH - 8, NCH - 4):
                embed(j, j // 2, j % 2, False, j < NCH - 5, True)
            done = [0]

            def prep(ins):
                done[0] += 1
                ins.then_inc(s_prep2, 1)
                pool.wait_ge(s_prep2, done[0])

            g = nc.gpsimd
            pool.wait_ge(s_lstm, 16 * 10)
            for j in (UD, WDF, WDB, WO):
                n = D if j == WO else 4 * H
                prep(g.tensor_scalar(raw[:, j, 0:n], raw[:, j, 0:n], S / HS, None, ALU.mult))
                prep(g.tensor_copy(hi[:, j, 0:n], raw[:, j, 0:n]))
                prep(g.tensor_tensor(lo[:, j, 0:n], raw[:, j, 0:n], hi[:, j, 0:n], ALU.subtract))
            pool.wait_ge(s_small, 16 * 12)
            pool.wait_ge(s_zero, 2)
            prep(g.tensor_scalar(brow[:, DEC_B, :], brow[:, DEC_B, :], S, None, ALU.mult))
            prep(g.tensor_copy(bp_hi[:, 2:4, :], brow[:, 2:4, :]))
            prep(g.tensor_tensor(brest[:, 2:4, :], brow[:, 2:4, :], bp_hi[:, 2:4, :], ALU.subtract))
            prep(g.tensor_copy(bp_mid[:, 2:4, :], brest[:, 2:4, :]))
            prep(g.tensor_copy(bpart[0:1, 2:4, :], bp_hi[0:1, 2:4, :]))
            prep(g.tensor_copy(bpart[32:33, 2:4, :], bp_mid[32:33, 2:4, :]))
            prep(g.tensor_tensor(bpart[64:65, 2:4, :], brest[64:65, 2:4, :], bp_mid[64:65, 2:4, :], ALU.subtract))
            assert done[0] == PREP2, done[0]

            def ffn(i):
                pool.wait_ge(f_ve, i + 1)
                nc.gpsimd.tensor_tensor(rstd[:], ve[:], halfneg[:], ALU.pow).then_inc(f_rstd, 1)
                pool.wait_ge(f_route[1], i + 1)
                nc.gpsimd.tensor_tensor(ex[:], ebase[:], dl[:], ALU.pow).then_inc(f_ex, 1)

            with pool.Fori(0, NCH) as i:
                ffn(i)

        def place(d, s):
            return s % SEED if d == 0 else SEED - 1 - s % SEED

        def act_step(d, s, zi_, zf_, af_, ai_, ao_, n):
            a = nc.scalar
            k = place(d, s)
            z = z_igo[d][s // SEED][:, k * 3 * B:(k + 1) * 3 * B]
            a.wait_ge(zf_, n)
            a.activation(gf[d][:], z_f[d][:, k * B:(k + 1) * B], ACT.Sigmoid, scale=1 / S).then_inc(af_, 1)
            a.wait_ge(zi_, n)
            a.activation(gi[d][:, :, 1], z[:, 0:B], ACT.Sigmoid, scale=1 / S)
            a.activation(gfc[d][:, :, 0], z[:, B:2 * B], ACT.Tanh, scale=1 / S).then_inc(ai_, 1)
            a.activation(go[d][:], z[:, 2 * B:3 * B], ACT.Sigmoid, scale=1 / S).then_inc(ao_, 1)

        def act_cell(d, at_, dc_, n):
            nc.scalar.wait_ge(dc_, n)
            nc.scalar.activation(tc[d][:], cs[d][:, :, 1], ACT.Tanh).then_inc(at_, 1)

        @block.scalar
        def _(act):
            act.wait_ge(dh[1], 1)
            nc.scalar.activation(tc[0][:], h32[1][:], ACT.Sigmoid).then_inc(ao[1], 1)
            def embed(h, r, q, t, x):
                c = r + SEED * q
                if t:
                    if h == 3:
                        act.wait_ge(e_t4, c + SEED * 7)
                        if not isinstance(c, int) or c > -SEED * LEAD:
                            act.wait_ge(e_split, c + SEED * 6)
                        if not isinstance(c, int) or c > -SEED * (LEAD - 1):
                            act.wait_ge(e_conv, c + SEED * 5)
                        nc.scalar.activation(rowsT[0:D, 4 * P:5 * P], pB[0:D, 0:P], ACT.Copy, scale=SX)
                        nc.scalar.activation(rT_hi[0:D, q, 4 * P:5 * P], pB[0:D, 0:P], ACT.Copy, scale=SX).then_inc(e_r4, SEED)
                    if h == 5:
                        act.wait_ge(e_tr, c + SEED * 7)
                        nc.scalar.activation(rowsT[:, 0:2 * P], pA[:, 0:2 * P], ACT.Copy, scale=SX)
                        nc.scalar.activation(rT_hi[:, q, 0:P], pA[:, 0:P], ACT.Copy, scale=SX)
                    if h == 6:
                        nc.scalar.activation(rT_hi[:, q, P:3 * P], pA[:, P:3 * P], ACT.Copy, scale=SX)
                        nc.scalar.activation(rowsT[:, 2 * P:3 * P], pA[:, 2 * P:3 * P], ACT.Copy, scale=SX)
                    if h == 7:
                        nc.scalar.activation(rowsT[:, 3 * P:4 * P], pA[:, 3 * P:4 * P], ACT.Copy, scale=SX)
                        nc.scalar.activation(rT_hi[:, q, 3 * P:4 * P], pA[:, 3 * P:4 * P], ACT.Copy, scale=SX).then_inc(e_evac, SEED)
                if x and h == 4:
                    col = r * (P // STEPS) + 3 * P if q else (NCH - 1) * P - r * (P // STEPS)
                    act.wait_ge(e_xnT, c + SEED * 4)
                    nc.scalar.activation(xT[:, bass.ds(col, P)], pB[:, P:P + P // 2].bitcast(F16), ACT.Copy).then_inc(e_xT, SEED)

            def pair(i, t, x):
                for s in range(STEPS):
                    for d in range(2):
                        act_step(d, s, zi[d], zf[d], af[d], ai[d], ao[d], i + s + 1)
                        embed(2 * (s % SEED) + d, i, s // SEED, t, x[s // SEED])
                        act_cell(d, at[d], dc[d], i + s + 1)

            act.wait_ge(s_const, 4)
            for j in range(-LEAD, 0):
                for h in range(8):
                    embed(h, j // 2 * STEPS, j % 2, True, j >= -3)
                if j == -5:
                    act.wait_ge(s_lstm, 16 * 10)
                    for k in (UF, UB, WF, WB):
                        nc.scalar.activation(raw[:, k, :], raw[:, k, :], ACT.Copy, scale=S / HS if k in (UF, UB) else S).then_inc(s_scaled, 1)
                    act.wait_ge(s_scaled, 4)
                    for k in (UF, UB, WF, WB):
                        nc.scalar.activation(hi[:, k, :], raw[:, k, :], ACT.Copy).then_inc(s_scaled, 1)
            with act.Fori(0, T // 2 - 4 * STEPS, BODY * STEPS) as i:
                for k in range(BODY):
                    pair(i + k * STEPS, True, (True, True))
            pair(T // 2 - 4 * STEPS, True, (True, True))
            pair(T // 2 - 3 * STEPS, False, (True, True))
            pair(T // 2 - 2 * STEPS, False, (True, False))
            pair(T // 2 - STEPS, False, (False, False))
            with act.Fori(T // 2, T, BODY * STEPS) as i:
                for k in range(BODY):
                    pair(i + k * STEPS, False, (False, False))

            def relu1(i, j):
                if j == PAIRS:
                    act.wait_ge(f_l1, i + 1)
                nc.scalar.activation(g1[:, j, :], pB[:, j * P:(j + 1) * P], ACT.Relu).then_inc(f_g1[j], 1)

            def relu2(i, j):
                if j == 0:
                    act.wait_ge(f_l2, i + 1)
                nc.scalar.activation(g2[:, j, :], pC[:, j * P:(j + 1) * P], ACT.Relu, bias=b2[:, j:j + 1]).then_inc(f_g2[j], 1)

            def chunk(i, steps, first, second):
                for s in range(STEPS):
                    if steps:
                        act_step(0, s, dzi, dzf, daf, dai, dao, i * STEPS + s + 1)
                    if first and s == 7:
                        relu2(i - 1, 0)
                        relu2(i - 1, 1)
                    if steps:
                        act_cell(0, dat, ddc, i * STEPS + s + 1)
                    if second and s == 1:
                        act.wait_ge(f_route[7], i - 1)
                        nc.scalar.activation(wt0[:], pd[:], ACT.Sigmoid, scale=-1.0)
                        nc.scalar.activation(wt1[:], pd[:], ACT.Sigmoid).then_inc(f_wt, 1)
                    if first:
                        if s == 2:
                            act.wait_ge(f_tr, i)
                            nc.scalar.activation(fxT[:], pA[:, P:2 * P], ACT.Copy).then_inc(f_fxT, 1)
                        if s == 4:
                            relu1(i - 1, PAIRS)
                            relu1(i - 1, 0)
                        if s == 5:
                            relu1(i - 1, 1)
                            relu1(i - 1, 2)
                        if s == 7:
                            relu2(i - 1, 2)

            chunk(0, True, False, False)
            chunk(1, True, True, False)
            chunk(2, True, True, True)
            with act.Fori(3, NCH) as i:
                chunk(i, True, True, True)
            chunk(NCH, False, True, True)
            chunk(NCH + 1, False, False, True)

        def mm(o, l, r, start=False):
            return nc.tensor.matmul(o, l, r, start=start, stop=True, skip_group_check=True)

        def z_of(d, r, half, k, n=1):
            if r < 3:
                v = z_igo[d][half][:, 0:SEED * 3 * B].rearrange("p (k c) -> p k c", c=3 * B)
                return v[:, k:k + n, r * B:(r + 1) * B]
            return z_f[d][:, k * B:(k + n) * B].rearrange("p (k c) -> p k c", c=B)

        def recur(d, uj, s, zi_, zf_, dhi_, dlo_, n):
            gate = [slice(g * H, (g + 1) * H) for g in ORDER]
            z = [z_of(d, r, s // SEED, place(d, s)) for r in range(4)]
            prev = (s - 1) % STEPS
            nc.tensor.wait_ge(dhi_, n)
            for r in range(4):
                mm(z[r], hi[:, uj, gate[r]], hhi[d][:, prev, :])
                mm(z[r], lo[:, uj, gate[r]], hhi[d][:, prev, :])
            nc.tensor.wait_ge(dlo_, n)
            mm(z[3], hi[:, uj, gate[3]], hlo[d][:, prev, :]).then_inc(zf_, 1)
            for r in range(3):
                last = mm(z[r], hi[:, uj, gate[r]], hlo[d][:, prev, :])
            last.then_inc(zi_, 1)

        def seed_input(d, r, half, col):
            x = xT[:, bass.ds(col, SEED * B)]
            cols = slice(ORDER[r] * H, (ORDER[r] + 1) * H)
            z = z_of(d, r, half, 0, SEED)
            mm(z, bpart[:, ENC_B[d], cols], ones[:, 0:SEED * B], start=r in (0, 3))
            mm(z, hi[:, WF + d, cols], x)
            mm(z, lo[:, WF + d, cols], x)

        def seed_const(part, half):
            if part < 2:
                igo = z_igo[0][half][:, 0:SEED * 3 * B].rearrange("p (k c) -> p k c", c=3 * B)
                mm(igo, ident16[:], (zc_hi, zc_lo)[part][:, :, 0:3 * B], start=part == 0)
            else:
                f = z_f[0][:, 0:SEED * B].rearrange("p (k c) -> p k c", c=B)
                mm(f, ident16[:], zc_hi[:, :, 3 * B:4 * B], start=True)
                mm(f, ident16[:], zc_lo[:, :, 3 * B:4 * B])

        @block.tensor
        def _(pe):
            PRODUCTS = [(m, k) for m in range(NK) for k in range(3)]

            def embed(h, i, q, t, c, x):
                if not (t or c or x):
                    return
                j = i * 2 + q
                later = not isinstance(j, int)
                if h == 2 and (later or j > -5):
                    pe.wait_ge(e_hx, SEED * (j + 5 if later else min(j + 5, NCH)))
                if x and h == 2:
                    pe.wait_ge(e_xn, SEED * (j + 4))
                    nc.tensor.transpose(pB[:, P:P + P // 2].bitcast(F16), xn[:], ident16[:]).then_inc(e_xnT, SEED)
                if t and h < 5:
                    if h == 0:
                        pe.wait_ge(s_rows[q], i * 16 + 64)
                        if later or j > -LEAD:
                            pe.wait_ge(e_evac, SEED * (j + 6))
                    if h == 2:
                        nc.tensor.transpose(pB[0:D, 0:P], rows[:, q, (NK - 1) * P:GK], ident[:]).then_inc(e_t4, SEED)
                    else:
                        m = h if h < 2 else h - 1
                        tr = nc.tensor.transpose(pA[:, m * P:(m + 1) * P], rows[:, q, m * P:(m + 1) * P], ident[:])
                        if h == 4:
                            tr.then_inc(e_tr, SEED)
                if c and h >= 5:
                    if h == 5:
                        pe.wait_ge(e_split, SEED * (j + 6))
                        if t:
                            pe.wait_ge(e_r4, SEED * (j + 7))
                        if x:
                            pe.wait_ge(e_xT, SEED * (j + 4))
                    for m, k in PRODUCTS[(h - 5) * 5:(h - 4) * 5]:
                        rows_k = D if m == NK - 1 else P
                        last = mm(pB[:, 2 * P:2 * P + D], (rT_hi[:, 1 - q, :], rT_hi[:, 1 - q, :], rT_lo[:])[k][0:rows_k, m * P:(m + 1) * P],
                                  (cw_hi, cw_lo, cw_hi)[k][0:rows_k, m, :], start=(m, k) == (0, 0))
                    if h == 7:
                        last.then_inc(e_conv, SEED)

            def pair(i, t, c, x):
                for s in range(STEPS):
                    n = i * STEPS + s + 1
                    half = s // SEED
                    hs = 2 * (s % SEED)
                    if s == SEED and x[0]:
                        pe.wait_ge(e_xT, SEED * (i * 2 + 4))
                    recur(0, UF, s, zi[0], zf[0], dhi[0], dlo[0], n)
                    if s % SEED == 0:
                        pe.wait_ge(ao[1], n)
                        seed_input(1, 3, half, (NCH - i) * P + (1 - half) * SEED * B)
                    else:
                        seed_input(1, s % SEED - 1, 1 - half, (NCH - i) * P - half * SEED * B)
                    embed(hs, i, half, t, c[half], x[half])
                    recur(1, UB, s, zi[1], zf[1], dhi[1], dlo[1], n)
                    if s % SEED == SEED - 1:
                        pe.wait_ge(ao[0], n)
                    seed_input(0, s % SEED, 1 - half, i * P + (P + (half + 1) * SEED * B))
                    embed(hs + 1, i, half, t, c[half], x[half])

            pe.wait_ge(s_const, 2)
            for j in range(-LEAD, 0):
                if j == -5:
                    pe.wait_ge(s_cw, 6)
                if j == -3:
                    pe.wait_ge(s_const, 6)
                for h in range(8):
                    embed(h, j // 2, j % 2, True, j >= -5, j >= -3)
            pe.wait_ge(s_prep, PREP)
            pe.wait_ge(s_const, 9)
            for d in range(2):
                for g in range(4 if d == 0 else 3):
                    seed_input(d, g, 0, P if d == 0 else NCH * P + SEED * B)
            with pe.Fori(0, (NCH // 2 - 4) // BODY) as i:
                for k in range(BODY):
                    pair(BODY * i + k, True, (True, True), (True, True))
            pair(NCH // 2 - 4, True, (True, True), (True, True))
            pair(NCH // 2 - 3, False, (True, False), (True, True))
            pair(NCH // 2 - 2, False, (False, False), (True, False))
            pair(NCH // 2 - 1, False, (False, False), (False, False))
            with pe.Fori(NCH // 2 // BODY, NCH // BODY) as i:
                for k in range(BODY):
                    pair(BODY * i + k, False, (False, False), (False, False))
            pe.wait_ge(s_prep2, PREP2)
            for d in range(2):
                pe.wait_ge(dhi[d], T + 1)
                pe.wait_ge(dlo[d], T + 1)
            for r, g in enumerate(ORDER):
                cols = slice(g * H, (g + 1) * H)
                o = pA[:, r * B:(r + 1) * B]
                mm(o, bpart[:, DEC_B, cols], ones[:, 0:B], start=r == 0)
                for d in range(2):
                    mm(o, hi[:, WDF + d, cols], hhi[d][:, STEPS - 1, :])
                    mm(o, lo[:, WDF + d, cols], hhi[d][:, STEPS - 1, :])
                    last = mm(o, hi[:, WDF + d, cols], hlo[d][:, STEPS - 1, :])
            last.then_inc(s_zc, 1)
            pe.wait_ge(s_zcs, 3)
            for part in range(3):
                seed_const(part, 0)

            def l1(i, j):
                if j == PAIRS:
                    pe.wait_ge(f_fxT, i + 1)
                m = mm(pB[:, j * P:(j + 1) * P], w1[:, j, :], fxT[:], start=True)
                if j == PAIRS - 1:
                    m.then_inc(f_l1, 1)

            def chunk(i, steps, first, second):
                for s in range(STEPS):
                    if steps:
                        n = i * STEPS + s + 1
                        recur(0, UD, s, dzi, dzf, ddhi, ddlo, n)
                        if s % SEED < 2:
                            seed_const(s % SEED, 1 - s // SEED)
                    if first:
                        if s == 0:
                            if not steps:
                                pe.wait_ge(ddlo, i * STEPS + 1)
                            h_hi = hhi[0][:].rearrange("p s b -> p (s b)")
                            h_lo = hlo[0][:].rearrange("p s b -> p (s b)")
                            mm(pA[:, 0:D], h_hi, hi[:, WO, 0:D], start=True)
                            mm(pA[:, 0:D], h_hi, lo[:, WO, 0:D])
                            mm(pA[:, 0:D], h_lo, hi[:, WO, 0:D]).then_inc(f_proj, 1)
                        if s == 2:
                            pe.wait_ge(f_fx, i)
                            nc.tensor.transpose(pA[:, P:2 * P], fx[:], ident[:]).then_inc(f_tr, 1)
                        if s == 3:
                            l1(i - 1, PAIRS)
                            l1(i - 1, 0)
                        if s == 4:
                            l1(i - 1, 1)
                            l1(i - 1, 2)
                        if s == 5:
                            pe.wait_ge(f_g1[PAIRS], i)
                            mm(pA[:, 3 * P:3 * P + NPAD], g1[:, PAIRS, :], wr2[:], start=True).then_inc(f_lg, 1)
                            pe.wait_ge(f_g1[0], i)
                            mm(pC[:, 0:P], w2[:, 0, :], g1[:, 0, :], start=True)
                        if s == 6:
                            pe.wait_ge(f_g1[2], i)
                            mm(pC[:, P:2 * P], w2[:, 1, :], g1[:, 1, :], start=True)
                            mm(pC[:, 2 * P:3 * P], w2[:, 2, :], g1[:, 2, :], start=True).then_inc(f_l2, 1)
                    if second:
                        if s == 0:
                            if not (isinstance(i, int) and i == 2):
                                pe.wait_ge(f_comb[NE - 1], i - 2)
                            mm(pD[:, 0:NE * D], ones[:], bpart[:, E3_B, 0:NE * D], start=True)
                            pe.wait_ge(f_g2[PAIRS - 1], i - 1)
                            mm(pD[:, 0:P], g2[:, 0, :], w3[:, 0, :])
                        if s == 1:
                            mm(pD[:, P:2 * P], g2[:, 1, :], w3[:, 1, :])
                            mm(pD[:, 2 * P:3 * P], g2[:, 2, :], w3[:, 2, :]).then_inc(f_l3, 1)
                    if steps and s % SEED == SEED - 1:
                        pe.wait_ge(dao, n)
                        seed_const(2, None)

            pe.wait_ge(s_ffw, FFW)
            pe.wait_ge(s_const, 19)
            chunk(0, True, False, False)
            chunk(1, True, True, False)
            chunk(2, True, True, True)
            with pe.Fori(3, NCH) as i:
                chunk(i, True, True, True)
            chunk(NCH, False, True, True)
            chunk(NCH + 1, False, False, True)

        @block.vector
        def _(dve):
            v = nc.vector
            done = [0]

            def prep(ins, chain=True):
                done[0] += 1
                ins.then_inc(s_prep, 1)
                if chain:
                    dve.wait_ge(s_prep, done[0])

            def wait_apart(count, n):
                dve.wait_ge(s_ids, 16)
                dve.wait_ge(count, n)

            dve.wait_ge(s_ids, 16)
            v.tensor_scalar(idx_f[:], idx_in[:], float(-HALF), float(VOCAB - 1 + HALF), ALU.max, ALU.min).then_inc(s_idx, 1)
            dve.wait_ge(s_idx, 1)
            v.tensor_scalar(idx_f[:], idx_f[:], float(PAD - HALF), None, ALU.add).then_inc(s_idx, 1)
            dve.wait_ge(s_idx, 2)
            v.tensor_copy(idx[:], idx_f[:]).then_inc(s_idx, 1)
            v.memset(brow[:], 0.0).then_inc(s_zero, 1)
            v.memset(bpart[:], 0.0).then_inc(s_zero, 1)
            for d in range(2):
                if d == 1:
                    v.memset(h32[d][:], 0.0).then_inc(dh[d], 1)
                prep(v.memset(gi[d][:], 0.0), False)
                prep(v.memset(cs[d][:], 0.0), False)
                if d == 0:
                    v.memset(hlo[d][:], 0.0).then_inc(dlo[d], 1)
                v.memset(hhi[d][:], 0.0).then_inc(dhi[d], 1)
            dve.wait_ge(s_conv, 64)
            for m, k in ((slice(0, NK - 1), P), (slice(NK - 1, NK), D)):
                v.tensor_scalar(convw[0:k, m, :], convw[0:k, m, :], SW, None, ALU.mult).then_inc(s_cw, 1)
            dve.wait_ge(s_cw, 2)
            for m, k in ((slice(0, NK - 1), P), (slice(NK - 1, NK), D)):
                v.tensor_copy(cw_hi[0:k, m, :], convw[0:k, m, :]).then_inc(s_cw, 1)
            dve.wait_ge(s_cw, 4)
            for m, k in ((slice(0, NK - 1), P), (slice(NK - 1, NK), D)):
                v.tensor_tensor(cw_lo[0:k, m, :], convw[0:k, m, :], cw_hi[0:k, m, :], ALU.subtract).then_inc(s_cw, 1)

            def embed(h, r, q, steps):
                c = r + SEED * (q + 5)
                if h == 0:
                    dve.wait_ge(e_conv, c)
                    v.scalar_tensor_tensor(out=hx[:], in0=pB[:, 2 * P:2 * P + D], scalar=1 / (SX * SW), in1=convb[:],
                                           op0=ALU.mult, op1=ALU.add).then_inc(e_hx, SEED)
                if h == 1:
                    if not steps:
                        dve.wait_ge(e_hx, c)
                    v.bn_stats(st[:], hx[:]).then_inc(e_st, SEED)
                if h == 2:
                    if not steps:
                        dve.wait_ge(e_st, c)
                    v.bn_aggr(mv[:], st[:]).then_inc(e_mv, SEED)
                if h == 3:
                    if not steps:
                        dve.wait_ge(e_mv, c)
                    v.tensor_scalar(ve[:], mv[:, 1:2], EPS, None, ALU.add).then_inc(e_ve, SEED)
                if h == 5:
                    dve.wait_ge(e_rstd, c)
                    v.tensor_scalar(xn32[:], hx[:], mv[:, 0:1], rstd[:], ALU.subtract, ALU.mult).then_inc(e_xn32, SEED)
                if h == 6:
                    if not isinstance(c, int) or c > SEED:
                        dve.wait_ge(e_xnT, c - SEED)
                    if not steps:
                        dve.wait_ge(e_xn32, c)
                    v.tensor_copy(xn[:, 0:D], xn32[:]).then_inc(e_xn, SEED // 2)
                if h == 7:
                    if not steps:
                        dve.wait_ge(e_xn, c - SEED // 2)
                    v.tensor_tensor(xn[:, D:2 * D], xn32[:], xn[:, 0:D], ALU.subtract).then_inc(e_xn, SEED // 2)

            EB = slice(0, 2)
            for j in range(-4, 0):
                for h in range(8):
                    embed(h, j // 2 * STEPS, j % 2, False)
                    if h == 3 and j == -3:
                        dve.wait_ge(s_small, 16 * 12)
                        dve.wait_ge(s_zero, 2)
                        prep(v.tensor_scalar(brow[:, EB, :], brow[:, EB, :], S, None, ALU.mult), False)
                    if h == 3 and j == -2:
                        dve.wait_ge(s_prep, done[0])
                        prep(v.tensor_copy(bp_hi[:, EB, :], brow[:, EB, :]), False)
                    if h == 3 and j == -1:
                        dve.wait_ge(s_prep, done[0])
                        prep(v.tensor_tensor(brest[:, EB, :], brow[:, EB, :], bp_hi[:, EB, :], ALU.subtract), False)
                if j == -4:
                    dve.wait_ge(s_scaled, 2 * 4)
                k = (UF, UB, WF, WB)[j + 4]
                prep(v.tensor_tensor(lo[:, k, :], raw[:, k, :], hi[:, k, :], ALU.subtract), False)
            dve.wait_ge(s_prep, done[0])
            prep(v.tensor_copy(bp_mid[:, EB, :], brest[:, EB, :]), False)
            prep(v.tensor_copy(bpart[0:1, EB, :], bp_hi[0:1, EB, :]), False)
            dve.wait_ge(s_prep, done[0] - 1)
            prep(v.tensor_copy(bpart[32:33, EB, :], bp_mid[32:33, EB, :]), False)
            prep(v.tensor_tensor(bpart[64:65, EB, :], brest[64:65, EB, :], bp_mid[64:65, EB, :], ALU.subtract), False)
            assert done[0] == PREP, done[0]

            def forget(d, af_, dp_, n):
                dve.wait_ge(af_, n)
                v.tensor_tensor(gfc[d][:, :, 1], gf[d][:], cs[d][:, :, 1], ALU.mult).then_inc(dp_, 1)

            def cell(d, dp_, ai_, dc_, n):
                dve.wait_ge(dp_, n)
                dve.wait_ge(ai_, n)
                v.tensor_tensor_scan(cs[d][:].rearrange("p b k -> p (b k)"), gi[d][:].rearrange("p b k -> p (b k)"),
                                     gfc[d][:].rearrange("p b k -> p (b k)"), 0.0, ALU.mult, ALU.add).then_inc(dc_, 1)

            def hidden(d, s, at_, dhi_, dh_, n):
                dve.wait_ge(at_, n)
                v.scalar_tensor_tensor(out=hhi[d][:, s, :], in0=go[d][:], scalar=HS, in1=tc[d][:],
                                       op0=ALU.mult, op1=ALU.mult).then_inc(dhi_, 1)
                v.scalar_tensor_tensor(out=h32[d][:], in0=go[d][:], scalar=HS, in1=tc[d][:],
                                       op0=ALU.mult, op1=ALU.mult).then_inc(dh_, 1)

            def low(d, s, dh_, dlo_, n):
                dve.wait_ge(dh_, n)
                v.tensor_tensor(hlo[d][:, s, :], h32[d][:], hhi[d][:, s, :], ALU.subtract).then_inc(dlo_, 1)

            def pair(i, norm):
                for s in range(STEPS):
                    n = i + s + 1
                    for d in range(2):
                        forget(d, af[d], dp[d], n)
                        if d == 0:
                            low(1, (s - 1) % STEPS, dh[1], dlo[1], n)
                        else:
                            low(0, s, dh[0], dlo[0], n)
                        cell(d, dp[d], ai[d], dc[d], n)
                        if norm:
                            embed(2 * (s % SEED) + d, i, s // SEED, True)
                        hidden(d, s, at[d], dhi[d], dh[d], n)

            with dve.Fori(0, T // 2 - 4 * STEPS, BODY * STEPS) as i:
                for k in range(BODY):
                    pair(i + k * STEPS, True)
            for k in (4, 3, 2, 1):
                pair(T // 2 - k * STEPS, k > 2)
            with dve.Fori(T // 2, T, BODY * STEPS) as i:
                for k in range(BODY):
                    pair(i + k * STEPS, False)
            dve.wait_ge(e_h1, SEED * NCH)
            dve.wait_ge(s_const, 19)
            low(1, STEPS - 1, dh[1], dlo[1], T + 1)

            dve.wait_ge(s_zc, 1)
            v.tensor_copy(zc32[:], pA[:, 0:4 * B]).then_inc(s_zcs, 1)
            dve.wait_ge(s_zcs, 1)
            zc_b = zc32[:].rearrange("p (a c) -> p a c", a=1).broadcast_to([P, SEED, 4 * B])
            v.tensor_copy(zc_hi[:], zc_b).then_inc(s_zcs, 1)
            dve.wait_ge(s_zcs, 2)
            v.memset(cs[0][:], 0.0).then_inc(s_prep, 1)
            v.memset(hlo[0][:], 0.0).then_inc(ddlo, 1)
            v.memset(hhi[0][:], 0.0).then_inc(ddhi, 1)
            v.tensor_tensor(zc_lo[:], zc_b, zc_hi[:], ALU.subtract).then_inc(s_zcs, 1)
            dve.wait_ge(s_prep, PREP + 1)

            def route(n, k, apart=False):
                (wait_apart if apart else dve.wait_ge)(f_route[k - 2], n)

            def chunk(i, steps, first, second):
                for s in range(STEPS):
                    n = i * STEPS + s + 1
                    if steps:
                        forget(0, daf, ddp, n)
                        cell(0, ddp, dai, ddc, n)
                    a, b = i - 1, i - 2
                    if first:
                        if s == 1:
                            wait_apart(f_st, i)
                            v.bn_aggr(mv[:], st[:]).then_inc(f_mv, 1)
                        if s == 2:
                            dve.wait_ge(f_rstd, i)
                            v.tensor_scalar(fx[:, 0:D], y1[:], mv[:, 0:1], rstd[:], ALU.subtract, ALU.mult).then_inc(f_fx, 1)
                        if s == 7:
                            v.tensor_copy(yres[:], y1[:]).then_inc(f_yres, 1)
                        if s == 6:
                            route(i, 2)
                            v.tensor_scalar(dl[:], pA[:, 3 * P:3 * P + NPAD], m8[:, 0:1], None, ALU.subtract).then_inc(f_route[1], 1)
                        if s == 7:
                            dve.wait_ge(f_ex, i)
                            v.tensor_reduce(exs[:], ex[:], mybir.AxisListType.X, ALU.add).then_inc(f_exs, 1)
                    if second:
                        if s == 0:
                            if first:
                                dve.wait_ge(f_proj, i)
                            route(i - 1, 4)
                            v.tensor_scalar(pr[:], ex[:], exr[:], None, ALU.mult).then_inc(f_route[3], 1)
                        if s == 1:
                            route(i - 1, 6)
                            v.tensor_tensor(pd[:], p8[:, 1:2], p8[:, 0:1], ALU.subtract).then_inc(f_route[7], 1)
                        if s == 2:
                            route(i - 1, 7)
                            v.tensor_copy(topf[:], top[:]).then_inc(f_route[6], 1)
                        if s == 3:
                            route(i - 1, 8)
                            dve.wait_ge(f_wt, i - 1)
                            v.tensor_scalar(rw0[:], iota[:], topf[:, 0:1], wt0[:], ALU.is_equal, ALU.mult).then_inc(f_route[8], 1)
                        if 4 <= s < 7:
                            comb(b, 2 * (s - 4))
                    if steps:
                        if s == 0 and first and not second:
                            dve.wait_ge(f_proj, i)
                        hidden(0, s, dat, ddhi, ddh, n)
                        low(0, s, ddh, ddlo, n)
                    if second and s == 0:
                        route(i - 1, 5, apart=True)
                        v.max(p8[:], pr[:]).then_inc(f_route[4], 1)
                    if second:
                        if s == 1:
                            v.max_index(top[:], p8[:], pr[:]).then_inc(f_route[5], 1)
                        if s == 3:
                            v.tensor_scalar(rw1[:], iota[:], topf[:, 1:2], wt1[:], ALU.is_equal, ALU.mult).then_inc(f_route[9], 1)
                            route(i - 1, 11)
                            v.tensor_tensor(rw[:], rw0[:], rw1[:], ALU.add).then_inc(f_route[10], 1)
                        if 4 <= s < 7:
                            comb(b, 2 * (s - 4) + 1)
                    if first:
                        if s == 0:
                            dve.wait_ge(f_proj, i)
                            if second:
                                dve.wait_ge(f_yres, i - 1)
                            v.scalar_tensor_tensor(out=y1[:], in0=pA[:, 0:D], scalar=1 / S,
                                                   in1=h1[:, bass.ds(a, 1), :].rearrange("p c d -> p (c d)"),
                                                   op0=ALU.mult, op1=ALU.add).then_inc(f_y1, 1)
                            dve.wait_ge(f_y1, i)
                            v.bn_stats(st[:], y1[:]).then_inc(f_st, 1)
                        if s == 1:
                            dve.wait_ge(f_mv, i)
                            v.tensor_scalar(ve[:], mv[:, 1:2], EPS, None, ALU.add).then_inc(f_ve, 1)
                        if s == 7:
                            dve.wait_ge(f_exs, i)
                            v.reciprocal(exr[:], exs[:]).then_inc(f_route[2], 1)
                        if s == 5:
                            wait_apart(f_lg, i)
                            v.max(m8[:], pA[:, 3 * P:3 * P + NPAD]).then_inc(f_route[0], 1)

            def comb(b, e):
                if e == 0:
                    dve.wait_ge(f_l3, b + 1)
                    dve.wait_ge(f_route[ROUTE - 1], b + 1)
                    dve.wait_ge(f_yres, b + 1)
                else:
                    dve.wait_ge(f_comb[e - 1], b + 1)
                if e == NE - 1 and not (isinstance(b, int) and b == 0):
                    dve.wait_ge(s_out, 16 * b)
                v.scalar_tensor_tensor(out=yout[:] if e == NE - 1 else acc[:], in0=pD[:, e * D:(e + 1) * D],
                                       scalar=rw[:, e:e + 1], in1=yres[:] if e == 0 else acc[:],
                                       op0=ALU.mult, op1=ALU.add).then_inc(f_comb[e], 1)

            chunk(0, True, False, False)
            chunk(1, True, True, False)
            chunk(2, True, True, True)
            with dve.Fori(3, NCH) as i:
                chunk(i, True, True, True)
            chunk(NCH, False, True, True)
            chunk(NCH + 1, False, False, True)


ROUTE = 11
PREP = 4 + 4 + 7
PREP2 = 3 * 4 + 7

_IN = ["L0_tok_b", "L0_attn_Wf", "L0_attn_Uf", "L0_attn_bf", "L0_attn_Wb", "L0_attn_Ub", "L0_attn_bb",
       "L0_attn_Wd", "L0_attn_Ud", "L0_attn_bd", "L0_attn_Wo", "L0_attn_bo", "L0_ffn_router_w1",
       "L0_ffn_router_b1", "L0_ffn_router_w2", "L0_ffn_router_b2", "L0_ffn_expert_w1", "L0_ffn_expert_b1",
       "L0_ffn_expert_w2", "L0_ffn_expert_b2", "L0_ffn_expert_w3", "L0_ffn_expert_b3"]


def kernel(**inputs):
    import numpy as np
    import concourse.bacc as bacc
    from concourse.bass_utils import run_bass_kernel_spmd as run

    nc = bacc.Bacc("TRN2", target_bir_lowering=False, num_devices=1)
    a = {k: np.ascontiguousarray(inputs[k]) for k in _IN}
    a["ids"] = np.ascontiguousarray(np.asarray(inputs["x"]).reshape(B, NCH, STEPS).transpose(2, 0, 1).reshape(P, NCH))
    emb = np.asarray(inputs["L0_tok_emb"])
    a["table"] = np.concatenate([np.repeat(emb[:1], PAD, axis=0), emb, np.repeat(emb[-1:], PAD, axis=0)])
    a["L0_ffn_expert_b2"] = np.ascontiguousarray(a["L0_ffn_expert_b2"].reshape(PAIRS, P).T)
    a["conv_w"] = np.ascontiguousarray(np.asarray(inputs["L0_tok_W"]).transpose(2, 1, 0))
    t = {k: nc.dram_tensor("in_" + k, x.shape, mybir.dt.from_np(x.dtype), kind="ExternalInput").ap() for k, x in a.items()}
    o = nc.dram_tensor("out_h", (B, T, D), F32, kind="ExternalOutput").ap()
    at = lambda n: t["L0_attn_" + n]
    ff = lambda n: t["L0_ffn_" + n]
    tower(nc, t["ids"], t["table"], t["conv_w"], t["L0_tok_b"], (at("Wf"), at("Wb")), (at("Uf"), at("Ub")),
          (at("bf"), at("bb")), at("Wd"), at("Ud"), at("bd"), at("Wo"), at("bo"),
          ff("router_w1"), ff("router_b1"), ff("router_w2"), ff("router_b2"), ff("expert_w1"), ff("expert_b1"),
          ff("expert_w2"), ff("expert_b2"), ff("expert_w3"), ff("expert_b3"), o)
    r = run(nc, [{"in_" + k: x for k, x in a.items()}], core_ids=[0])
    return r.results[0]["out_h"]
```
